# Optimizing a Trainium2 kernel written in Bass

```python
import numpy as np
import jax
import jax.numpy as jnp

def _softmax(x, axis=-1):
    return jax.nn.softmax(x, axis=axis)

def _gelu(x):
    return jax.nn.gelu(x, approximate=True)

def _silu(x):
    return jax.nn.silu(x)

def _sigmoid(x):
    return jax.nn.sigmoid(x)

def _layernorm(x, axis=-1, eps=1e-05):
    m = jnp.mean(x, axis=axis, keepdims=True)
    v = jnp.var(x, axis=axis, keepdims=True)
    return (x - m) / jnp.sqrt(v + eps)

def _scatter_add(tgt, idx, src, axis=0):
    return tgt.at[idx].add(src)

def _segment_sum(src, seg, n):
    return jax.ops.segment_sum(src, seg, n)
kernel_name = 'mk_gnn_ffn_d1_gnn_r32_0b92a2'

def setup_inputs(seed: int=0):
    np.random.seed(seed)
    _w = jnp.asarray

    def _rec_inputs():
        import jax
        import jax.numpy as jnp
        _gk = jax.random.key(seed)
        x = -0.0002117 + 1 * jax.random.normal(jax.random.fold_in(_gk, 1), (3125, 256), jnp.float32)
        src = jax.random.randint(jax.random.fold_in(_gk, 2), (50000,), 0, 3125, jnp.int32)
        dst = jnp.minimum((3125 * jax.random.uniform(jax.random.fold_in(_gk, 3), (50000,)) ** 2.0).astype(jnp.int32), 99999)
        _o = jnp.argsort(dst, stable=True)
        src = src[_o]
        dst = dst[_o]
        edge_weight = jax.random.uniform(jax.random.fold_in(_gk, 12), (50000,), jnp.float32, 0.0, 1)
        return (x, src, dst, edge_weight)
    x, src, dst, edge_weight = _rec_inputs()

    def _L0_gnn_setup():
        import jax, jax.numpy as jnp
        import numpy as np
        N_NODES = 3125
        N_EDGES = 100000
        D_IN = 256
        D_OUT = 256
        key = jax.random.key(seed)
        k1, k2, k3, k4, k5 = jax.random.split(key, 5)
        x = jax.random.normal(k1, (N_NODES, D_IN), dtype=jnp.float32)
        edge_row = jax.random.randint(k2, (N_EDGES,), 0, N_NODES, dtype=jnp.int32)
        edge_col = jax.random.randint(k3, (N_EDGES,), 0, N_NODES, dtype=jnp.int32)
        edge_val = jax.random.uniform(k4, (N_EDGES,), dtype=jnp.float32)
        limit = 1.414 * np.sqrt(6.0 / (D_IN + D_OUT))
        weight = jax.random.uniform(k5, (D_IN, D_OUT), dtype=jnp.float32, minval=-limit, maxval=limit)
        b = jnp.zeros((D_OUT,), dtype=jnp.float32)
        return {'x': x, 'edge_row': edge_row, 'edge_col': edge_col, 'edge_val': edge_val, 'weight': weight, 'b': b}
    _L0_gnn_all = _L0_gnn_setup()
    _L0_gnn_in = {k: v for k, v in _L0_gnn_all.items() if k in ('weight', 'b')}
    del _L0_gnn_all

    def _L0_ffn_setup():
        import jax, jax.numpy as jnp
        import numpy as np
        NUM_EXPERTS = 8
        TOP_K = 2
        B, S, D = (8, 256, 256)

        def _moe(tokens, router_w, w1, b1, w2, b2):
            N = tokens.shape[0]
            E = router_w.shape[0]
            logits = tokens.astype(jnp.float32) @ router_w.astype(jnp.float32).T
            probs = jax.nn.softmax(logits, axis=-1)
            rw, re = jax.lax.top_k(probs, TOP_K)
            if TOP_K > 1:
                rw = rw / jnp.maximum(rw.sum(-1, keepdims=True), 1e-12)
            rw = rw.astype(tokens.dtype)
            combine = jnp.zeros((N, E), tokens.dtype).at[jnp.arange(N)[:, None], re].set(rw)
            out = tokens
            for e in range(E):
                h = jax.nn.gelu(tokens @ w1[e] + b1[e], approximate=False)
                y = h @ w2[e] + b2[e]
                out = out + combine[:, e:e + 1] * y
            return out
        key = jax.random.key(seed)
        ks = jax.random.split(key, 4)
        scale = 1.0 / np.sqrt(D).astype(np.float32)
        return {'input_embeddings': jax.random.normal(ks[0], (B, S, D), jnp.float32), 'router_w': jax.random.normal(ks[1], (NUM_EXPERTS, D), jnp.float32) * scale, 'w1': jax.random.normal(ks[2], (NUM_EXPERTS, D, D), jnp.float32) * scale, 'b1': jnp.zeros((NUM_EXPERTS, D), jnp.float32), 'w2': jax.random.normal(ks[3], (NUM_EXPERTS, D, D), jnp.float32) * scale, 'b2': jnp.zeros((NUM_EXPERTS, D), jnp.float32)}
    _L0_ffn_all = _L0_ffn_setup()
    _L0_ffn_in = {k: v for k, v in _L0_ffn_all.items() if k in ('router_w', 'w1', 'b1', 'w2', 'b2')}
    del _L0_ffn_all
    return {'x': x, 'src': src, 'dst': dst, 'edge_weight': edge_weight, 'L0_gnn_weight': _L0_gnn_in['weight'], 'L0_gnn_b': _L0_gnn_in['b'], 'L0_ffn_router_w': _L0_ffn_in['router_w'], 'L0_ffn_w1': _L0_ffn_in['w1'], 'L0_ffn_b1': _L0_ffn_in['b1'], 'L0_ffn_w2': _L0_ffn_in['w2'], 'L0_ffn_b2': _L0_ffn_in['b2']}

def reference(x, src, dst, edge_weight, L0_gnn_weight, L0_gnn_b, L0_ffn_router_w, L0_ffn_w1, L0_ffn_b1, L0_ffn_w2, L0_ffn_b2):
    import jax
    import jax.numpy as jnp

    def _L0_gnn_ref(x, edge_row, edge_col, edge_val, weight, b):
        import jax, jax.numpy as jnp
        import numpy as np
        N_NODES = 3125
        N_EDGES = 100000
        D_IN = 256
        D_OUT = 256
        h = jnp.matmul(x, weight)
        msgs = edge_val[:, None] * h[edge_col]
        out = jax.ops.segment_sum(msgs, edge_row, num_segments=N_NODES)
        return out + b

    def _L0_ffn_ref(input_embeddings, router_w, w1, b1, w2, b2):
        import jax, jax.numpy as jnp
        import numpy as np
        NUM_EXPERTS = 8
        TOP_K = 2
        B, S, D = (8, 256, 256)

        def _moe(tokens, router_w, w1, b1, w2, b2):
            N = tokens.shape[0]
            E = router_w.shape[0]
            logits = tokens.astype(jnp.float32) @ router_w.astype(jnp.float32).T
            probs = jax.nn.softmax(logits, axis=-1)
            rw, re = jax.lax.top_k(probs, TOP_K)
            if TOP_K > 1:
                rw = rw / jnp.maximum(rw.sum(-1, keepdims=True), 1e-12)
            rw = rw.astype(tokens.dtype)
            combine = jnp.zeros((N, E), tokens.dtype).at[jnp.arange(N)[:, None], re].set(rw)
            out = tokens
            for e in range(E):
                h = jax.nn.gelu(tokens @ w1[e] + b1[e], approximate=False)
                y = h @ w2[e] + b2[e]
                out = out + combine[:, e:e + 1] * y
            return out
        b, s, d = input_embeddings.shape
        tokens = input_embeddings.reshape(b * s, d)
        return _moe(tokens, router_w, w1, b1, w2, b2).reshape(b, s, d)
    x = x + _L0_gnn_ref(_layernorm(x, axis=-1), src, dst, edge_weight, L0_gnn_weight, L0_gnn_b)
    x = x + _L0_ffn_ref(_layernorm(x, axis=-1)[None], L0_ffn_router_w, L0_ffn_w1, L0_ffn_b1, L0_ffn_w2, L0_ffn_b2)[0]
    return x

_drawn_inputs = setup_inputs


def setup_inputs(seed=0):
    import zlib

    import numpy as np

    out = dict(_drawn_inputs(seed))
    spreads = {'L0_gnn_b': (0.0, 0.1), 'L0_ffn_b1': (0.0, 0.701), 'L0_ffn_b2': (0.0, 0.476)}
    factors = {}
    for name, (base, spread) in spreads.items():
        noise = np.random.default_rng([zlib.crc32(name.encode()), seed]).standard_normal(out[name].shape)
        drawn = base * np.exp(spread * noise) if base else spread * noise
        out[name] = jnp.asarray(drawn.astype(out[name].dtype))
    for name, factor in factors.items():
        out[name] = (out[name] * factor).astype(out[name].dtype)
    return out
```

```python
import concourse.bass as bass
from concourse import mybir
from contextlib import ExitStack


BLOCKS = 25
CHUNKS = 17


def room(edges):
    cap = CHUNKS * 128
    return cap, -(-(edges - cap) // 128) + BLOCKS - 1


def build_gnn_moe(nc, x, src, dst, edge_weight, gnn_w, gnn_b, router_w, w1, b1, w2, b2,
                  out, rec_dram, h_dram):
    fp32 = mybir.dt.float32
    i32 = mybir.dt.int32
    u32 = mybir.dt.uint32
    u8 = mybir.dt.uint8
    ALU = mybir.AluOpType
    ACT = mybir.ActivationFunctionType
    AX = mybir.AxisListType

    P = 128
    N, D = x.shape
    E = src.shape[0]
    CAP, OV = room(E)
    NE = router_w.shape[0]
    KC = D // P
    NB = BLOCKS
    BN = N // NB
    EC = -(-E // P)
    EL = E - (P - 1) * EC
    CH = CAP // P
    OV0 = NB * CAP
    ROWS = (OV0 + OV * P) // P
    LB = -(-N // P)
    LR = N - (LB - 1) * P
    MAGIC = 12582912.0

    with ExitStack() as ctx:
        def sb(name, shape, dt=fp32):
            return ctx.enter_context(nc.sbuf_tensor(name, shape, dt))

        def pb(name, shape, dt=fp32):
            return ctx.enter_context(nc.psum_tensor(name, shape, dt))

        def sem(name):
            return ctx.enter_context(nc.semaphore(name))

        ident = sb("ident", [P, P])
        lower = sb("lower", [P, P])
        ones = sb("ones", [P, P])
        iota_row = sb("iota_row", [P, P])
        src_i = sb("src_i", [P, EC], i32)
        dst_i = sb("dst_i", [P, EC], i32)
        ew = sb("ew", [P, EC])
        srcf = sb("srcf", [P, EC])
        blk = sb("blk", [P, EC])
        onehot = sb("onehot", [P, NB, EC], mybir.dt.float16)
        rank = sb("rank", [P, 2, EC])
        posf = sb("posf", [P, EC])
        pos = sb("pos", [P, EC], i32)
        rec = sb("rec", [P, EC, 4])
        rowcnt = sb("rowcnt", [P, NB])
        rowbase = sb("rowbase", [P, NB])
        total = sb("total", [P, NB])
        ovc = sb("ovc", [P, NB])
        ovend = sb("ovend", [P, NB])
        delta = sb("delta", [P, NB])
        nov = sb("nov", [P, 1], i32)
        ovf = sb("ovf", [P, EC])
        ovblk = sb("ovblk", [1, OV])
        ovblk_i = sb("ovblk_i", [1, OV], i32)
        ovnum = sb("ovnum", [1, OV])
        recov = sb("recov", [P, 4])

        xt = sb("xt", [P, LB, D])
        xpb = sb("xpb", [P, NB, D])
        gw = sb("gw", [P, KC, D])
        gb_row = sb("gb_row", [1, D])
        gb = sb("gb", [P, D])
        rw_n = sb("rw_n", [NE, D])
        rwT = sb("rwT", [P, KC, NE])
        w1s = sb("w1s", [P, NE, KC, D])
        w2s = sb("w2s", [P, NE, KC, D])
        b1n = sb("b1n", [NE * KC, P])
        b1T = sb("b1T", [P, NE * KC])
        b2s = sb("b2s", [NE, D])

        st = sb("st", [P, 2, 6])
        mv = sb("mv", [P, 2, 2])
        rstd = sb("rstd", [P, 2, 1])
        tmp1 = sb("tmp1", [P, 2, 1])
        stx = sb("stx", [P, LB, 6])
        mvx = sb("mvx", [P, LB, 2])
        varx = sb("varx", [P, LB])
        meanx = sb("meanx", [P, LB])
        rsx = sb("rsx", [P, LB])
        tmpx = sb("tmpx", [P, LB])
        ones_e = rec[:, :, 3]
        xh = sb("xh", [P, 2, D])
        xhT = sb("xhT", [P, 2, KC, P])
        hs = sb("hs", [P, 2, D])

        recb = sb("recb", [P, 2, CH * 4])
        S = sb("S", [P, 2, CH, P])
        G = sb("G", [P, CH, D])
        zero = G[:, :, :].rearrange("p c d -> p (c d)")[:, 0:ROWS * 4]
        x1 = sb("x1", [P, 2, D])
        x2 = sb("x2", [P, 2, D])
        x2T = sb("x2T", [P, 2, KC, P])
        acc = sb("acc", [P, 2, D])
        hT = sb("hT", [P, 2, KC, P])
        sm = sb("sm", [P, 2, 64])
        lg = sb("lg", [P, 2, NE])
        idx8 = sb("idx8", [P, 2, 8], u32)
        combT = sb("combT", [NE, 2, P])

        pagg = [pb(f"pagg{i}", [P, 512]) for i in range(2)]
        ptr = pb("ptr", [P, 512])
        pmisc = pb("pmisc", [P, 512])
        ph = [pb(f"ph{i}", [P, 512]) for i in range(2)]
        py = [pb(f"py{i}", [P, 512]) for i in range(2)]

        s_turn = sem("s_turn")
        s_fix = sem("s_fix")
        s_edges = sem("s_edges")
        s_x = sem("s_x")
        s_xpb = sem("s_xpb")
        s_w = sem("s_w")
        s_pool0 = sem("s_pool0")
        s_const = sem("s_const")
        s_ms = sem("s_ms")
        s_zero = sem("s_zero")
        s_dve = sem("s_dve")
        s_cnt = sem("s_cnt")
        s_base = sem("s_base")
        s_pos = sem("s_pos")
        s_scat = sem("s_scat")
        s_setT = sem("s_setT")
        s_setC = sem("s_setC")
        s_xh = sem("s_xh")
        s_xhT = sem("s_xhT")
        s_xhTc = sem("s_xhTc")
        s_hp = sem("s_hp")
        s_hc = sem("s_hc")
        s_hst = [sem(f"s_hst{i}") for i in range(2)]
        s_xpbready = sem("s_xpbready")

        s_nov = sem("s_nov")
        s_ovrec = sem("s_ovrec")
        s_ovS = sem("s_ovS")
        s_ovG = sem("s_ovG")
        s_ovmm = sem("s_ovmm")
        s_ovadd = sem("s_ovadd")
        s_rec = [sem(f"s_rec{i}") for i in range(2)]
        s_G = [sem(f"s_G{i}") for i in range(CH)]
        s_S = sem("s_S")
        s_mm = sem("s_mm")
        s_x1 = sem("s_x1")
        s_x2 = sem("s_x2")
        s_x2T = sem("s_x2T")
        s_x2Tc = sem("s_x2Tc")
        s_lg = sem("s_lg")
        s_mx = sem("s_mx")
        s_lgc = sem("s_lgc")
        s_ex = sem("s_ex")
        s_comb = sem("s_comb")
        s_cT = sem("s_cT")
        s_cTc = sem("s_cTc")
        s_yb = sem("s_yb")
        s_h1 = sem("s_h1")
        s_gelu = sem("s_gelu")
        s_y = sem("s_y")
        s_yacc = sem("s_yacc")
        s_out = [sem(f"s_out{i}") for i in range(2)]

        block = ctx.enter_context(nc.Block())

        def pairs(eng, body, first=0, last=NB):
            b = first
            while b < 2 or b % 2:
                body(b, b % 2)
                b += 1
            turns = (last - b) // 2
            if turns:
                with eng.Fori(0, turns) as i:
                    body(i * 2 + b, 0)
                    body(i * 2 + (b + 1), 1)
            b += 2 * turns
            if b < last:
                body(b, 0)

        def apart(eng):
            eng.sem_inc(s_turn, 1)

        def wait(eng, s, n):
            if not isinstance(n, int) or n > 0:
                eng.wait_ge(s, n)

        class Chain:
            def __init__(self, eng):
                self.eng, self.base, self.n = eng, 0, 0

            def __call__(self, ins):
                self.n += 1
                ins.then_inc(s_dve, 1)
                self.eng.wait_ge(s_dve, self.base + self.n)

        @block.sync
        def _(sp):
            for tile, dram in ((src_i, src), (dst_i, dst), (ew, edge_weight)):
                if tile is src_i:
                    sp.wait_ge(s_ms, 3)
                sp.dma_start(tile[0:P - 1, :], dram[0:(P - 1) * EC].rearrange("(p f) -> p f", f=EC)).then_inc(s_edges, 16)
                sp.dma_start(tile[P - 1:P, 0:EL], dram[(P - 1) * EC:E].rearrange("(p f) -> p f", p=1)).then_inc(s_edges, 16)
            sp.wait_ge(s_ms, 5)
            sp.dma_start(xt[:, 0:LB - 1, :], x[0:(LB - 1) * P, :].rearrange("(b p) d -> p b d", p=P)).then_inc(s_x, 16)
            sp.dma_start(xt[0:LR, LB - 1, :], x[(LB - 1) * P:N, :]).then_inc(s_x, 16)
            sp.dma_start(gw[:, :, :], gnn_w.rearrange("(c k) n -> k c n", k=P)).then_inc(s_w, 16)
            sp.dma_start(gb_row[:, :], gnn_b.rearrange("(a n) -> a n", a=1)).then_inc(s_w, 16)
            sp.dma_start(rw_n[:, :], router_w).then_inc(s_w, 16)
            sp.dma_start(b1n[:, :], b1.rearrange("e (c k) -> (e c) k", k=P)).then_inc(s_w, 16)
            sp.dma_start(b2s[:, :], b2).then_inc(s_w, 16)
            sp.dma_start(w1s[:, :, :, :].rearrange("k e c n -> k (e c) n"), w1.rearrange("e (c k) n -> k (e c) n", k=P)).then_inc(s_w, 16)
            sp.dma_start(w2s[:, :, :, :].rearrange("k e c n -> k (e c) n"), w2.rearrange("e (c k) n -> k (e c) n", k=P)).then_inc(s_w, 16)
            sp.dma_start(xpb[0:BN, :, :], x.rearrange("(b p) d -> p b d", p=BN)).then_inc(s_xpb, 16)

            def store_h(b, q):
                sp.wait_ge(s_hc, b + 1)
                sp.dma_start(h_dram[bass.ds(b * P, P), :], hs[:, q, :]).then_inc(s_hst[q], 16)
            pairs(sp, store_h, last=LB)
            sp.wait_ge(s_scat, 16 * EC)

            sp.wait_ge(s_nov, 1)
            with sp.If(sp.value_load(nov[0:1, 0:1], min_val=0, max_val=OV) > 0):
                sp.dma_start(recov[:, :], rec_dram[bass.ds(OV0, P), :]).then_inc(s_ovrec, 16)
                with sp.Fori(1, OV) as j:
                    sp.wait_ge(s_ovadd, j)
                    sp.dma_start(recov[:, :], rec_dram[bass.ds(j * P + OV0, P), :]).then_inc(s_ovrec, 16)

            def load_rec(b, q):
                wait(sp, s_mm, CH * (b - 1))
                sp.dma_start(recb[:, q, :], rec_dram[bass.ds(b * CAP, CAP), :].rearrange("(p c) w -> p (c w)", p=P))\
                  .then_inc(s_rec[q], 16)

            def store_out(b, q):
                sp.wait_ge(s_yacc, (NE + 1) * (b + 1))
                sp.dma_start(out[bass.ds(b * BN, BN), :], acc[0:BN, q, :]).then_inc(s_out[q], 16)

            load_rec(0, 0)
            load_rec(1, 1)

            def step(b, q):
                store_out(b - 2, q)
                load_rec(b, q)
            def step(b, q):
                load_rec(b, q)
                if isinstance(b, int) and b - 3 < 0:
                    return
                store_out(b - 3, 1 - q)
            step(2, 0)
            pairs(sp, step, first=3)
            for b in range(NB - 3, NB):
                store_out(b, b % 2)
            sp.wait_ge(s_out[0], 16 * ((NB + 1) // 2))
            sp.wait_ge(s_out[1], 16 * (NB // 2))

        @block.gpsimd
        def _(pool):
            pool.memset(dst_i[:, :], 0).then_inc(s_ms, 1)
            pool.memset(ew[:, :], 0.0).then_inc(s_ms, 1)
            pool.memset(src_i[:, :], N).then_inc(s_ms, 1)
            pool.memset(xt[:, LB - 1, :], 0.0).then_inc(s_ms, 1)
            pool.memset(xpb[:, :, :], 0.0).then_inc(s_ms, 1)
            pool.memset(ident[:, :], 0.0).then_inc(s_pool0, 1)
            pool.memset(ones[:, :], 1.0).then_inc(s_pool0, 1)
            pool.memset(zero, 0.0).then_inc(s_pool0, 1)
            pool.iota(iota_row[:, :], pattern=[[1, P]], base=0, channel_multiplier=0,
                      allow_small_or_imprecise_dtypes=True).then_inc(s_pool0, 1)
            pool.iota(ovnum[:, :], pattern=[[1, OV]], base=0, channel_multiplier=0,
                      allow_small_or_imprecise_dtypes=True).then_inc(s_pool0, 1)
            pool.wait_ge(s_pool0, 5)
            pool.affine_select(out=ident[:, :], in_=ident[:, :], compare_op=ALU.not_equal, fill=1.0,
                               base=0, pattern=[[-1, P]], channel_multiplier=1).then_inc(s_const, 1)
            pool.affine_select(out=lower[:, :], in_=ones[:, :], compare_op=ALU.is_gt, fill=0.0,
                               base=0, pattern=[[1, P]], channel_multiplier=-1).then_inc(s_const, 1)
            pool.dma_start(rec_dram.rearrange("(p r) w -> p (r w)", p=P), zero).then_inc(s_zero, 16)
            pool.wait_ge(s_zero, 16)
            pool.wait_ge(s_pos, 1)
            for f in range(EC):
                n = P if f < EL else P - 1
                pool.indirect_dma_start(rec_dram[:, :], bass.IndirectOffsetOnAxis(ap=pos[0:n, f:f + 1], axis=0),
                                        rec[0:n, f, :], None).then_inc(s_scat, 16)
            pool.wait_ge(s_hst[0], 16 * ((LB + 1) // 2))
            pool.wait_ge(s_hst[1], 16 * (LB // 2))

            pool.wait_ge(s_nov, 1)
            with pool.If(pool.value_load(nov[0:1, 0:1], min_val=0, max_val=OV) > 0):
                with pool.Fori(0, OV) as j:
                    pool.wait_ge(s_ovrec, j * 16 + 16)
                    apart(pool)
                    pool.indirect_dma_start(
                        G[:, 0, :], None, h_dram[:, :],
                        bass.IndirectOffsetOnAxis(ap=recov[:, 0:1].bitcast(i32), axis=0)).then_inc(s_ovG, 16)
                    pool.wait_ge(s_ovmm, j + 1)
                    apart(pool)
                pool.wait_ge(s_ovmm, OV)

            def gather(b, q):
                pool.wait_ge(s_rec[q], ((b - q) * 8 + 16) if isinstance(b, int) else (b - q) * 8 + 16)
                for c in range(CH):
                    if c in (0, CH // 2):
                        wait(pool, s_mm, CH * (b - 1) + (CH // 2 if c == 0 else CH))
                        apart(pool)
                    pool.indirect_dma_start(
                        G[:, c, :], None, h_dram[:, :],
                        bass.IndirectOffsetOnAxis(ap=recb[:, q, 4 * c:4 * c + 1].bitcast(i32), axis=0)).then_inc(s_G[c], 16)
            gather(0, 0)
            pairs(pool, gather, first=1)

        @block.vector
        def _(dve):
            chain = Chain(dve)
            v = nc.vector

            def rsqrt_steps(y, var, t):
                chain(v.tensor_scalar(var, var, 1e-5, None, ALU.add))
                chain(v.tensor_single_scalar(t.bitcast(i32), var.bitcast(i32), 1, ALU.arith_shift_right))
                chain(v.tensor_scalar(y.bitcast(i32), t.bitcast(i32), -1.0, 1597463007.0, ALU.mult, ALU.add))
                for _ in range(3):
                    chain(v.tensor_tensor(t, y, y, ALU.mult))
                    chain(v.scalar_tensor_tensor(t, t, -0.5, var, ALU.mult, ALU.mult))
                    chain(v.scalar_tensor_tensor(y, t, 1.5, y, ALU.add, ALU.mult))
            RS = 12
            dve.wait_ge(s_edges, 96)
            dve.wait_ge(s_const, 2)
            chain(v.tensor_copy(srcf[:, :], src_i[:, :]))
            chain(v.tensor_scalar(posf[:, :], srcf[:, :], 1.0 / BN, -(BN - 1) / (2.0 * BN), ALU.mult, ALU.add))
            chain(v.tensor_scalar(blk[:, :], posf[:, :], MAGIC, MAGIC, ALU.add, ALU.subtract))
            v.scalar_tensor_tensor(rec[:, :, 1], blk[:, :], -float(BN), srcf[:, :], ALU.mult, ALU.add)
            v.tensor_copy(rec[:, :, 0].bitcast(i32), dst_i[:, :])
            v.tensor_copy(rec[:, :, 2], ew[:, :])
            v.memset(ones_e, 1.0)
            for b in range(NB):
                last = v.tensor_scalar(onehot[:, b, :], blk[:, :], float(b), 0.0, ALU.is_equal, ALU.add,
                                       accum_out=rowcnt[:, b:b + 1])
            last.then_inc(s_cnt, 1)
            chain(v.memset(posf[:, :], 0.0))
            dve.wait_ge(s_base, 1)
            for b in range(NB):
                ins = v.tensor_scalar(rowbase[:, b:b + 1], pmisc[:, b:b + 1], float(b * CAP - 1), None, ALU.add)
            v.tensor_scalar(total[:, :], pmisc[:, 32:32 + NB], float(-CAP), 0.0, ALU.add, ALU.max)
            chain(v.tensor_copy(delta[:, :], pmisc[:, 32:32 + NB]))
            chain(v.tensor_scalar(ovc[:, :], total[:, :], 1.0 / P, 0.5 - 0.5 / P, ALU.mult, ALU.add))
            chain(v.tensor_scalar(ovc[:, :], ovc[:, :], MAGIC, MAGIC, ALU.add, ALU.subtract))
            chain(v.tensor_tensor_scan(ovend[:, :], ones[:, 0:NB], ovc[:, :], 0.0, ALU.mult, ALU.add))
            v.tensor_copy(nov[:, :], ovend[:, NB - 1:NB]).then_inc(s_nov, 1)
            for b in range(NB):
                chain(v.tensor_tensor_scan(rank[:, b % 2, :], ones_e, onehot[:, b, :], rowbase[:, b:b + 1],
                                           ALU.mult, ALU.add))
                v.copy_predicated(posf[:, :], onehot[:, b, :].bitcast(mybir.dt.int16), rank[:, b % 2, :])
            chain(v.memset(st[:, 0, :], 0.0))
            dve.wait_ge(s_nov, 1)

            with dve.If(dve.value_load(nov[0:1, 0:1], min_val=0, max_val=OV) > 0):
                n = [0]

                def fix(ins):
                    n[0] += 1
                    ins.then_inc(s_fix, 1)
                    dve.wait_ge(s_fix, n[0])
                fix(v.tensor_tensor(delta[:, :], ovend[:, :], ovc[:, :], ALU.subtract))
                fix(v.tensor_scalar(delta[:, :], delta[:, :], float(P), float(OV0 - CAP), ALU.mult, ALU.add))
                fix(v.scalar_tensor_tensor(delta[:, :], iota_row[:, 0:NB], float(-CAP), delta[:, :], ALU.mult, ALU.add))
                fix(v.memset(ovf[:, :], 0.0))
                for b in range(NB):
                    fix(v.scalar_tensor_tensor(ovf[:, :], onehot[:, b, :], delta[:, b:b + 1], ovf[:, :], ALU.mult, ALU.add))
                fix(v.scalar_tensor_tensor(rank[:, 0, :], blk[:, :], float(-CAP), posf[:, :], ALU.mult, ALU.add))
                fix(v.scalar_tensor_tensor(rank[:, 1, :], rank[:, 0, :], float(CAP), ovf[:, :], ALU.is_ge, ALU.mult))
                fix(v.tensor_tensor(posf[:, :], posf[:, :], rank[:, 1, :], ALU.add))
                fix(v.memset(ovblk[:, :], 0.0))
                for b in range(NB - 1):
                    fix(v.scalar_tensor_tensor(ovblk[:, :], ovnum[:, :], ovend[0:1, b:b + 1], ovblk[:, :], ALU.is_ge, ALU.add))
                fix(v.tensor_copy(ovblk_i[:, :], ovblk[:, :]))
            v.tensor_copy(pos[:, :], posf[:, :]).then_inc(s_pos, 1)

            dve.wait_ge(s_x, 32)
            for b in range(LB):
                ins = v.bn_stats(stx[:, b, :], xt[:, b, :])
            chain(ins)
            for b in range(LB):
                ins = v.bn_aggr(mvx[:, b, :], stx[:, b, :])
            chain(ins)
            chain(v.tensor_copy(varx[:, :], mvx[:, :, 1]))
            v.tensor_copy(meanx[:, :], mvx[:, :, 0])
            rsqrt_steps(rsx[:, :], varx[:, :], tmpx[:, :])

            def norm(b, q):
                wait(dve, s_xhT, b - 1)
                v.tensor_scalar(xh[:, q, :], xt[:, b, :], meanx[:, bass.ds(b, 1)], rsx[:, bass.ds(b, 1)], ALU.subtract, ALU.mult)\
                 .then_inc(s_xh, 1)
            pairs(dve, norm, last=LB)
            dve.wait_ge(s_xpb, 16)
            dve.wait_ge(s_setC, 3)
            v.tensor_tensor(xpb[:, :, :], xpb[:, :, :], gb[:, None, :].to_broadcast([P, NB, D]), ALU.add)\
             .then_inc(s_xpbready, 1)
            dve.wait_ge(s_xpbready, 1)
            with dve.If(dve.value_load(nov[0:1, 0:1], min_val=0, max_val=OV) > 0):
                with dve.Fori(0, OV) as j:
                    dve.wait_ge(s_ovrec, j * 16 + 16)
                    v.tensor_scalar(S[:, 0, 0, :], iota_row[:, :], recov[:, 1:2], recov[:, 2:3], ALU.is_equal, ALU.mult)\
                     .then_inc(s_ovS, 1)
                    dve.wait_ge(s_ovmm, j + 1)
                    ob = dve.value_load(ovblk_i[0:1, bass.ds(j, 1)], min_val=0, max_val=NB - 1)
                    v.tensor_tensor(xpb[:, bass.ds(ob, 1), :].rearrange("p a d -> p (a d)"), pmisc[:, 0:D],
                                    xpb[:, bass.ds(ob, 1), :].rearrange("p a d -> p (a d)"), ALU.add).then_inc(s_ovadd, 1)
                    dve.wait_ge(s_ovadd, j + 1)
                dve.wait_ge(s_ovadd, OV)
            base1 = chain.n
            PRE, ROUT = 2 + RS, 8

            def select(b, q):
                dve.wait_ge(s_rec[q], (b - q) * 8 + 16)
                wait(dve, s_mm, CH * (b - 1))
                for c in range(CH):
                    v.tensor_scalar(S[:, q, c, :], iota_row[:, :], recb[:, q, 4 * c + 1:4 * c + 2],
                                    recb[:, q, 4 * c + 2:4 * c + 3], ALU.is_equal, ALU.mult).then_inc(s_S, 1)

            def pre(b, q):
                chain.base, chain.n = base1 + (PRE + ROUT) * b, 0
                dve.wait_ge(s_mm, CH * (b + 1))
                v.tensor_tensor(x1[:, q, :], pagg[q][:, 0:D], xpb[:, b, :], ALU.add).then_inc(s_x1, 1)
                dve.wait_ge(s_x1, b + 1)
                chain(v.bn_stats(st[:, q, :], x1[:, q, :]))
                apart(dve)
                chain(v.bn_aggr(mv[:, q, :], st[:, q, :]))
                rsqrt_steps(rstd[:, q, :], mv[:, q, 1:2], tmp1[:, q, :])
                v.tensor_scalar(x2[:, q, :], x1[:, q, :], mv[:, q, 0:1], rstd[:, q, :], ALU.subtract, ALU.mult)\
                 .then_inc(s_x2, 1)
                assert chain.n == PRE

            def route(b, q):
                chain.base, chain.n = base1 + (PRE + ROUT) * b + PRE, 0
                t = sm[:, q, :]
                dve.wait_ge(s_lgc, b + 1)
                v.reduce_max(t[:, 0:1], lg[:, q, :], AX.X, negate=True).then_inc(s_mx, 1)
                wait(dve, s_out[q], (b - q) * 8)
                chain(v.tensor_tensor(acc[:, q, :], x1[:, q, :], x2[:, q, :], ALU.add))
                dve.wait_ge(s_ex, b + 1)
                chain(v.reciprocal(t[:, 1:2], t[:, 2:3]))
                chain(v.tensor_scalar(t[:, 8:16], t[:, 16:24], t[:, 1:2], None, ALU.mult))
                apart(dve)
                chain(v.max(t[:, 24:32], t[:, 8:16]))
                apart(dve)
                v.max_index(idx8[:, q, :], t[:, 24:32], t[:, 8:16])
                chain(v.tensor_scalar(t[:, 3:4], t[:, 24:25], t[:, 25:26], 1e-12, ALU.add, ALU.max))
                v.tensor_copy(t[:, 4:6], idx8[:, q, 0:2])
                chain(v.reciprocal(t[:, 6:7], t[:, 3:4]))
                chain(v.tensor_scalar(t[:, 32:34], t[:, 24:26], t[:, 6:7], None, ALU.mult))
                v.tensor_scalar(t[:, 40:48], iota_row[:, 0:NE], t[:, 4:5], t[:, 32:33], ALU.is_equal, ALU.mult)
                chain(v.tensor_scalar(t[:, 48:56], iota_row[:, 0:NE], t[:, 5:6], t[:, 33:34], ALU.is_equal, ALU.mult))
                v.tensor_tensor(t[:, 56:64], t[:, 40:48], t[:, 48:56], ALU.add).then_inc(s_comb, 1)
                assert chain.n == ROUT, chain.n

            def experts(b, q):
                dve.wait_ge(s_comb, b + 1)
                for e in range(NE):
                    dve.wait_ge(s_y, NE * b + e + 1)
                    wait(dve, s_yacc, (NE + 1) * b + e)
                    v.scalar_tensor_tensor(acc[:, q, :], py[e % 2][:, 0:D], sm[:, q, 56 + e:57 + e], acc[:, q, :],
                                           ALU.mult, ALU.add).then_inc(s_yacc, 1)
                dve.wait_ge(s_yb, b + 1)
                dve.wait_ge(s_yacc, (NE + 1) * b + NE)
                v.tensor_tensor(acc[:, q, :], acc[:, q, :], pmisc[:, 256:512], ALU.add).then_inc(s_yacc, 1)

            select(0, 0)
            select(1, 1)
            pre(0, 0)

            def step(b, q):
                if not (isinstance(b, int) and b == NB - 1):
                    select(b + 1, 1 - q)
                route(b - 1, 1 - q)
                experts(b - 1, 1 - q)
                pre(b, q)
            pairs(dve, step, first=1, last=NB - 1)
            step(NB - 1, (NB - 1) % 2)
            route(NB - 1, (NB - 1) % 2)
            experts(NB - 1, (NB - 1) % 2)

        @block.scalar
        def _(act):
            a = nc.scalar
            act.wait_ge(s_setT, 1)
            a.copy(gb[:, :], ptr[:, 256:512]).then_inc(s_setC, 1)
            a.copy(rwT[:, :, :].rearrange("k c e -> k (c e)"), ptr[:, 64:64 + KC * NE]).then_inc(s_setC, 1)
            a.copy(b1T[:, :], ptr[:, 96:96 + NE * KC]).then_inc(s_setC, 1)

            def h_rows(b, q):
                act.wait_ge(s_xhT, b + 1)
                wait(act, s_hp, b - 1)
                a.copy(xhT[:, q, :, :].rearrange("k c n -> k (c n)"), ph[q][:, 0:KC * P]).then_inc(s_xhTc, 1)
                act.wait_ge(s_hp, b + 1)
                wait(act, s_hst[q], (b - q) * 8)
                a.copy(hs[:, q, :], py[q][:, 0:D]).then_inc(s_hc, 1)
            pairs(act, h_rows, last=LB)

            def ffn(b, q):
                act.wait_ge(s_x2T, b + 1)
                wait(act, s_h1, NE * (b - 1))
                a.copy(x2T[:, q, :, :].rearrange("k c n -> k (c n)"), ptr[:, 0:KC * P]).then_inc(s_x2Tc, 1)
                act.wait_ge(s_lg, b + 1)
                a.copy(lg[:, q, :], pmisc[:, 0:NE]).then_inc(s_lgc, 1)
                act.wait_ge(s_mx, b + 1)
                a.activation(sm[:, q, 16:24], lg[:, q, :], ACT.Exp, bias=sm[:, q, 0:1], scale=1.0,
                             accum_out=sm[:, q, 2:3]).then_inc(s_ex, 1)
                for e in range(NE):
                    act.wait_ge(s_h1, NE * b + e + 1)
                    wait(act, s_y, NE * b + e - 1)
                    for m in range(KC):
                        ins = a.activation(hT[:, e % 2, m, :], ph[e % 2][:, m * P:(m + 1) * P], ACT.Gelu,
                                           bias=b1T[:, e * KC + m:e * KC + m + 1], scale=1.0)
                    ins.then_inc(s_gelu, 1)
                act.wait_ge(s_cT, b + 1)
                a.copy(combT[:, q, :], ptr[0:NE, 256:256 + P]).then_inc(s_cTc, 1)
            pairs(act, ffn)

        @block.tensor
        def _(pe):
            t = nc.tensor
            pe.wait_ge(s_cnt, 1)
            pe.wait_ge(s_const, 2)
            t.matmul(pmisc[:, 0:NB], lhsT=lower[:, :], rhs=rowcnt[:, :], start=True, stop=True)
            t.matmul(pmisc[:, 32:32 + NB], lhsT=ones[:, :], rhs=rowcnt[:, :], start=True, stop=True).then_inc(s_base, 1)
            pe.wait_ge(s_w, 112)
            t.matmul(ptr[:, 256:512], lhsT=ones[0:1, :], rhs=gb_row[:, :], start=True, stop=True)
            for c in range(KC):
                t.transpose(ptr[:, 64 + c * NE:64 + (c + 1) * NE], rw_n[:, c * P:(c + 1) * P], ident[0:NE, 0:NE])
            t.transpose(ptr[:, 96:96 + NE * KC], b1n[:, :], ident[0:NE * KC, 0:NE * KC]).then_inc(s_setT, 1)

            def h_rows(b, q):
                pe.wait_ge(s_xh, b + 1)
                wait(pe, s_xhTc, b - 1)
                for c in range(KC):
                    ins = t.transpose(ph[q][:, c * P:(c + 1) * P], xh[:, q, c * P:(c + 1) * P], ident[:, :])
                ins.then_inc(s_xhT, 1)
                pe.wait_ge(s_xhTc, b + 1)
                wait(pe, s_hc, b - 1)
                for c in range(KC):
                    ins = t.matmul(py[q][:, 0:D], lhsT=xhT[:, q, c, :], rhs=gw[:, c, :], start=(c == 0), stop=(c == KC - 1))
                ins.then_inc(s_hp, 1)
            pairs(pe, h_rows, last=LB)

            def aggregate(b, q):
                wait(pe, s_x1, b - 1)
                for c in range(CH):
                    pe.wait_ge(s_S, CH * b + c + 1)
                    pe.wait_ge(s_G[c], (b + 1) * 16)
                    t.matmul(pagg[q][:, 0:D], lhsT=S[:, q, c, :], rhs=G[:, c, :], start=(c == 0), stop=(c == CH - 1))\
                     .then_inc(s_mm, 1)

            def ffn(b, q):
                pe.wait_ge(s_x2, b + 1)
                wait(pe, s_x2Tc, b)
                wait(pe, s_cTc, b)
                for c in range(KC):
                    ins = t.transpose(ptr[:, c * P:(c + 1) * P], x2[:, q, c * P:(c + 1) * P], ident[:, :])
                ins.then_inc(s_x2T, 1)
                pe.wait_ge(s_x2Tc, b + 1)
                wait(pe, s_yacc, (NE + 1) * b)
                for c in range(KC):
                    ins = t.matmul(pmisc[:, 0:NE], lhsT=x2T[:, q, c, :], rhs=rwT[:, c, :], start=(c == 0), stop=(c == KC - 1))
                ins.then_inc(s_lg, 1)

                def up(e):
                    wait(pe, s_gelu, NE * b + e - 1)
                    for m in range(KC):
                        for c in range(KC):
                            ins = t.matmul(ph[e % 2][:, m * P:(m + 1) * P], lhsT=w1s[:, e, c, m * P:(m + 1) * P],
                                           rhs=x2T[:, q, c, :], start=(c == 0), stop=(c == KC - 1))
                    ins.then_inc(s_h1, 1)

                def down(e):
                    pe.wait_ge(s_gelu, NE * b + e + 1)
                    if e >= 2:
                        pe.wait_ge(s_yacc, (NE + 1) * b + e - 1)
                    for m in range(KC):
                        ins = t.matmul(py[e % 2][:, 0:D], lhsT=hT[:, e % 2, m, :], rhs=w2s[:, e, m, :],
                                       start=(m == 0), stop=(m == KC - 1))
                    ins.then_inc(s_y, 1)

                up(0)
                for e in range(1, NE):
                    up(e)
                    down(e - 1)
                pe.wait_ge(s_comb, b + 1)
                t.transpose(ptr[0:NE, 256:256 + P], sm[:, q, 56:56 + NE], ident[:, :]).then_inc(s_cT, 1)
                down(NE - 1)
                pe.wait_ge(s_cTc, b + 1)
                t.matmul(pmisc[:, 256:512], lhsT=combT[:, q, :], rhs=b2s[:, :], start=True, stop=True).then_inc(s_yb, 1)

            pe.wait_ge(s_xpbready, 1)
            pe.wait_ge(s_setC, 3)
            pe.wait_ge(s_nov, 1)
            with pe.If(pe.value_load(nov[0:1, 0:1], min_val=0, max_val=OV) > 0):
                with pe.Fori(0, OV) as j:
                    pe.wait_ge(s_ovS, j + 1)
                    pe.wait_ge(s_ovG, j * 16 + 16)
                    t.matmul(pmisc[:, 0:D], lhsT=S[:, 0, 0, :], rhs=G[:, 0, :], start=True, stop=True).then_inc(s_ovmm, 1)
                    pe.wait_ge(s_ovadd, j + 1)
                pe.wait_ge(s_ovadd, OV)
            aggregate(0, 0)

            def step(b, q):
                aggregate(b, q)
                ffn(b - 1, 1 - q)
            pairs(pe, step, first=1)
            ffn(NB - 1, (NB - 1) % 2)


INPUTS = ["x", "src", "dst", "edge_weight", "L0_gnn_weight", "L0_gnn_b", "L0_ffn_router_w",
          "L0_ffn_w1", "L0_ffn_b1", "L0_ffn_w2", "L0_ffn_b2"]


def kernel(**inputs):
    import numpy as _np
    import concourse.bacc as _bacc
    from concourse import mybir as _mybir
    from concourse.bass_utils import run_bass_kernel_spmd as _run

    nc = _bacc.Bacc("TRN2", target_bir_lowering=False, num_devices=1)
    arrays, args = {}, []
    for name in INPUTS:
        a = _np.ascontiguousarray(inputs[name])
        arrays[f"in_{name}"] = a
        args.append(nc.dram_tensor(f"in_{name}", a.shape, _mybir.dt.from_np(a.dtype), kind="ExternalInput").ap())
    fp32 = _mybir.dt.float32
    out = nc.dram_tensor("out_0", (3125, 256), fp32, kind="ExternalOutput").ap()
    cap, beyond = room(arrays["in_src"].shape[0])
    rec = nc.dram_tensor("rec_scratch", (BLOCKS * cap + beyond * 128, 4), fp32, kind="Internal").ap()
    h = nc.dram_tensor("h_scratch", (3200, 256), fp32, kind="Internal").ap()
    build_gnn_moe(nc, *args, out, rec, h)
    r = _run(nc, [arrays], core_ids=[0])
    return r.results[0]["out_0"]
```

```python
import concourse.bass as bass
from concourse import mybir
from contextlib import ExitStack


BLOCKS = 25
CHUNKS = 17
SPAN = 56
CELL = 8


def room(edges):
    spans = -(-edges // (SPAN * 128))
    cap = CHUNKS * 128
    cells = (edges + spans * BLOCKS * (CELL - 1)) // CELL - cap // CELL
    return spans, cap, -(-cells * CELL // 128) + BLOCKS - 1, 1024


def build_gnn_moe(nc, x, src, dst, edge_weight, gnn_w, gnn_b, router_w, w1, b1, w2, b2,
                  out, rec_dram, h_dram):
    fp32 = mybir.dt.float32
    i32 = mybir.dt.int32
    u32 = mybir.dt.uint32
    f16 = mybir.dt.float16
    ALU = mybir.AluOpType
    ACT = mybir.ActivationFunctionType
    AX = mybir.AxisListType

    P = 128
    N, D = x.shape
    E = src.shape[0]
    NS, CAP, OV, SLOTC = room(E)
    NE = router_w.shape[0]
    KC = D // P
    NB = BLOCKS
    BN = N // NB
    SW = SPAN
    EC = NS * SW
    GR = SLOTC // P
    HI = GR * CELL
    BW = 7
    BT = SW // BW
    CH = CAP // P
    CAPC = CAP // CELL
    CC = P // CELL
    OV0 = NB * CAPC
    DUMP = OV0 + OV * CC
    CWORDS = 2 * CELL
    LB = -(-N // P)
    LR = N - (LB - 1) * P
    MAGIC = 12582912.0

    with ExitStack() as ctx:
        def sb(name, shape, dt=fp32):
            return ctx.enter_context(nc.sbuf_tensor(name, shape, dt))

        def pb(name, shape, dt=fp32):
            return ctx.enter_context(nc.psum_tensor(name, shape, dt))

        def sem(name):
            return ctx.enter_context(nc.semaphore(name))

        ident = sb("ident", [P, P])
        lower = sb("lower", [P, P])
        ones = sb("ones", [P, P])
        iota_row = sb("iota_row", [P, P])
        src_i = sb("src_i", [P, EC], i32)
        dst_i = sb("dst_i", [P, EC], i32)
        ew = sb("ew", [P, EC])
        srcf = sb("srcf", [P, EC])
        blk = sb("blk", [P, EC])
        onehot = sb("onehot", [P, NB, EC], f16)
        first_col = sb("first_col", [P, EC])
        rank = sb("rank", [P, 2, EC])
        posf = sb("posf", [P, EC])
        basef = sb("basef", [P, EC])
        slot = src_i[:, :]
        bits = [dst_i[:, :], rank[:, 0, :].bitcast(i32), rank[:, 1, :].bitcast(i32)]
        lanef = sb("lanef", [P, EC])
        hif = sb("hif", [P, EC])
        packf = sb("packf", [P, EC])
        cnt = sb("cnt", [P, NB, NS])
        cells = sb("cells", [P, NB, NS])
        cells_s = sb("cells_s", [P, NS, NB])
        not_span0 = sb("not_span0", [P, NB, NS])
        not_block0 = sb("not_block0", [P, NS, NB])
        upto_b = sb("upto_b", [P, NB, NS])
        upto_s = sb("upto_s", [P, NS, NB])
        first = sb("first", [P, NS, NB + 1])
        move = sb("move", [P, NS, NB + 1])
        movestep = sb("movestep", [P, NS, NB + 1])
        base = sb("base", [P, NS, NB])
        cellnum = sb("cellnum", [P, NS, GR])
        dump0 = sb("dump0", [P, NS])
        place = sb("place", [P, NS, GR])
        pick = sb("pick", [P, NS, GR])
        cellrow = sb("cellrow", [P, 2, GR, CELL, 2])
        placeof = sb("placeof", [P, 2, GR], i32)
        total = sb("total", [P, NB])
        ovc = sb("ovc", [P, NB])
        ovend = sb("ovend", [P, NB])
        behind = sb("behind", [P, NS, GR])
        deltastep = sb("deltastep", [P, NB + 1])
        delta = sb("delta", [P, 1, NB])
        nov = sb("nov", [P, 1], i32)
        ovblk = sb("ovblk", [1, OV])
        ovblk_i = sb("ovblk_i", [1, OV], i32)
        ovnum = sb("ovnum", [1, OV])
        recov = sb("recov", [P, 2])

        xt = sb("xt", [P, LB, D])
        xpb = sb("xpb", [P, NB, D])
        gw = sb("gw", [P, KC, D])
        gb_row = sb("gb_row", [1, D])
        gb = sb("gb", [P, D])
        rw_n = sb("rw_n", [NE, D])
        rwT = sb("rwT", [P, KC, NE])
        w1p = sb("w1p", [P, 2, NE, KC, D], f16)
        w2s = sb("w2s", [P, NE * KC, D])
        amax = sb("amax", [P, 3])
        amaxT = sb("amaxT", [3, 1])
        amaxd = sb("amaxd", [3, 3])
        pw = sb("pw", [P, 3])
        ipw = sb("ipw", [P, 3])
        fac = sb("fac", [P, 5])
        b1n = sb("b1n", [NE * KC, P])
        b1T = sb("b1T", [P, NE * KC])
        b2s = sb("b2s", [NE, D])

        st = sb("st", [P, 2, 6])
        mv = sb("mv", [P, 2, 2])
        rstd = sb("rstd", [P, 2, 1])
        tmp1 = sb("tmp1", [P, 2, 1])
        stx = sb("stx", [P, LB, 6])
        mvx = sb("mvx", [P, LB, 2])
        varx = sb("varx", [P, LB])
        meanx = sb("meanx", [P, LB])
        rsx = sb("rsx", [P, LB])
        tmpx = sb("tmpx", [P, LB])
        xh = sb("xh", [P, 2, D])
        xhT = sb("xhT", [P, 2, KC, P])
        hs = sb("hs", [P, 2, 2, D], f16)

        recb = sb("recb", [P, 2, CH, 2])
        packi = sb("packi", [P, 2, CH], i32)
        gidx = sb("gidx", [P, 2, CH], i32)
        rowi = sb("rowi", [P, 2, CH], i32)
        rowf = sb("rowf", [P, 2, CH])
        S = sb("S", [P, 2, CH, 2, P], f16)
        G = sb("G", [P, CH, 2, D], f16)
        w1s = G[:, :, :, :].rearrange("p c s d -> p (c s d)").bitcast(fp32)[:, 0:NE * KC * D]\
            .rearrange("p (a n) -> p a n", n=D)
        sort_room = S[:, :, :, :, :].rearrange("p a c s n -> p (a c s n)").bitcast(fp32)
        laneoh = sort_room[:, 0:2 * BW * P].rearrange("p (a c n) -> p a c n", a=2, n=P)
        moving = sort_room[:, 2 * BW * P:2 * BW * (P + 2 * HI)].rearrange("p (a c w n) -> p a c w n", a=2, w=2, n=HI)
        hioh = sb("hioh", [P, 2, BW, HI])
        at_least = sort_room[:, 0:NS * GR * (NB + 1)].rearrange("p (s g b) -> p s g b", s=NS, g=GR)
        steps = sort_room[:, NS * GR * (NB + 1):2 * NS * GR * (NB + 1)].rearrange("p (s g b) -> p s g b", s=NS, g=GR)
        zero = w1p[:, :, :, :, :].rearrange("p s e c n -> p (s e c n)").bitcast(fp32)[:, 0:DUMP * CWORDS // P]
        iota_h = sb("iota_h", [P, P], f16)
        wsc = sb("wsc", [P, 2, 3, CH])
        wh = sb("wh", [P, 2, CH], f16)
        x1 = sb("x1", [P, 2, D])
        x2 = sb("x2", [P, 2, D])
        x2T = sb("x2T", [P, 2, KC, P])
        x2p = sb("x2p", [P, 2, 2, KC, P], f16)
        acc = sb("acc", [P, 2, D])
        hT = sb("hT", [P, 2, KC, P])
        sm = sb("sm", [P, 2, 64])
        lg = sb("lg", [P, 2, NE])
        idx8 = sb("idx8", [P, 2, 8], u32)
        combT = sb("combT", [NE, 2, P])

        pagg = [pb(f"pagg{i}", [P, 512]) for i in range(2)]
        ptr = pb("ptr", [P, 512])
        pmisc = pb("pmisc", [P, 512])
        ph = [pb(f"ph{i}", [P, 512]) for i in range(2)]
        py = [pb(f"py{i}", [P, 512]) for i in range(2)]

        s_turn = sem("s_turn")
        s_fix = sem("s_fix")
        s_edges = sem("s_edges")
        s_x = sem("s_x")
        s_xpb = sem("s_xpb")
        s_w = sem("s_w")
        s_pool0 = sem("s_pool0")
        s_const = sem("s_const")
        s_ms = sem("s_ms")
        s_zero = sem("s_zero")
        s_dve = sem("s_dve")
        s_cnt = sem("s_cnt")
        s_base = sem("s_base")
        s_slots = sem("s_slots")
        s_hieq = sem("s_hieq")
        s_weighed = sem("s_weighed")
        s_packed = sem("s_packed")
        s_sorted = sem("s_sorted")
        s_cells = sem("s_cells")
        s_scat = [sem(f"s_scat{i}") for i in range(2)]
        s_gidx = sem("s_gidx")
        s_ovidx = sem("s_ovidx")
        s_setT = sem("s_setT")
        s_setC = sem("s_setC")
        s_xh = sem("s_xh")
        s_xhT = sem("s_xhT")
        s_xhTc = sem("s_xhTc")
        s_hp = sem("s_hp")
        s_hc = sem("s_hc")
        s_hst = [sem(f"s_hst{i}") for i in range(2)]
        s_xpbready = sem("s_xpbready")

        s_nov = sem("s_nov")
        s_sel = sem("s_sel")
        s_prep = sem("s_prep")
        s_rout = sem("s_rout")
        s_amax = sem("s_amax")
        s_amaxT = sem("s_amaxT")
        s_amaxd = sem("s_amaxd")
        s_amaxb = sem("s_amaxb")
        s_fac = sem("s_fac")
        s_scaled = sem("s_scaled")
        s_hi = sem("s_hi")
        s_split = sem("s_split")
        s_hlo = sem("s_hlo")
        s_ovw = sem("s_ovw")
        s_x2lo = sem("s_x2lo")
        s_ovrec = sem("s_ovrec")
        s_ovS = sem("s_ovS")
        s_ovG = sem("s_ovG")
        s_ovmm = sem("s_ovmm")
        s_ovadd = sem("s_ovadd")
        s_rec = [sem(f"s_rec{i}") for i in range(2)]
        s_G = [sem(f"s_G{i}") for i in range(CH)]
        s_S = sem("s_S")
        s_mm = sem("s_mm")
        s_x1 = sem("s_x1")
        s_x2 = sem("s_x2")
        s_x2T = sem("s_x2T")
        s_x2Tc = sem("s_x2Tc")
        s_lg = sem("s_lg")
        s_mx = sem("s_mx")
        s_lgc = sem("s_lgc")
        s_ex = sem("s_ex")
        s_comb = sem("s_comb")
        s_cT = sem("s_cT")
        s_cTc = sem("s_cTc")
        s_yb = sem("s_yb")
        s_h1 = sem("s_h1")
        s_gelu = sem("s_gelu")
        s_y = sem("s_y")
        s_yacc = sem("s_yacc")
        s_out = [sem(f"s_out{i}") for i in range(2)]

        block = ctx.enter_context(nc.Block())

        def pairs(eng, body, first=0, last=NB, steady=2):
            b = first
            while b < steady or b % 2:
                body(b, b % 2)
                b += 1
            turns = (last - b) // 2
            if turns:
                with eng.Fori(0, turns) as i:
                    body(i * 2 + b, 0)
                    body(i * 2 + (b + 1), 1)
            b += 2 * turns
            if b < last:
                body(b, 0)

        def added(e):
            return e if e < 2 else e + 1

        def apart(eng):
            eng.sem_inc(s_turn, 1)

        def wait(eng, s, n):
            if not isinstance(n, int) or n > 0:
                eng.wait_ge(s, n)

        def turns(eng, turn):
            turn(0, 0, True, False, False)
            turn(1, 1, True, True, False)
            pairs(eng, lambda b, q: turn(b, q, True, True, True), first=2, steady=4)
            turn(NB, NB % 2, False, True, True)
            turn(NB + 1, (NB + 1) % 2, False, False, True)

        SEL = 4

        class Chain:
            def __init__(self, eng, done):
                self.eng, self.done, self.base, self.n = eng, done, 0, 0
                self.between = None

            def __call__(self, ins):
                self.n += 1
                ins.then_inc(self.done, 1)
                if self.between:
                    self.between()
                self.eng.wait_ge(self.done, self.base + self.n)

        @block.sync
        def _(sp):
            full = (NS - 1) * P * SW
            rows = (E - full) // SW
            rest = E - full - rows * SW
            for tile, dram in ((src_i, src), (dst_i, dst), (ew, edge_weight)):
                if tile is src_i:
                    sp.wait_ge(s_ms, 3)
                by_span = tile[:, :].rearrange("p (s c) -> p s c", c=SW)
                sp.dma_start(by_span[:, 0:NS - 1, :], dram[0:full].rearrange("(s p c) -> p s c", p=P, c=SW)).then_inc(s_edges, 16)
                sp.dma_start(by_span[0:rows, NS - 1, :], dram[full:full + rows * SW].rearrange("(p c) -> p c", c=SW)).then_inc(s_edges, 16)
                sp.dma_start(by_span[rows:rows + 1, NS - 1, 0:rest], dram[full + rows * SW:E].rearrange("(p c) -> p c", p=1))\
                  .then_inc(s_edges, 16)
            sp.wait_ge(s_ms, 5)
            sp.dma_start(xt[:, 0:LB - 1, :], x[0:(LB - 1) * P, :].rearrange("(b p) d -> p b d", p=P)).then_inc(s_x, 16)
            sp.dma_start(xt[0:LR, LB - 1, :], x[(LB - 1) * P:N, :]).then_inc(s_x, 16)
            sp.dma_start(gw[:, :, :], gnn_w.rearrange("(c k) n -> k c n", k=P)).then_inc(s_w, 16)
            sp.dma_start(gb_row[:, :], gnn_b.rearrange("(a n) -> a n", a=1)).then_inc(s_w, 16)
            sp.dma_start(rw_n[:, :], router_w).then_inc(s_w, 16)
            sp.dma_start(b1n[:, :], b1.rearrange("e (c k) -> (e c) k", k=P)).then_inc(s_w, 16)
            sp.dma_start(b2s[:, :], b2).then_inc(s_w, 16)
            sp.dma_start(w1s, w1.rearrange("e (c k) n -> k (e c) n", k=P)).then_inc(s_w, 16)
            sp.dma_start(w2s[:, :, :], w2.rearrange("e (c k) n -> k (e c) n", k=P)).then_inc(s_w, 16)
            sp.dma_start(xpb[0:BN, :, :], x.rearrange("(b p) d -> p b d", p=BN)).then_inc(s_xpb, 16)

            def store_h(b, q):
                sp.wait_ge(s_hlo, b + 1)
                sp.dma_start(h_dram[bass.ds(b * P, P), :], hs[:, q, :, :].rearrange("p s d -> p (s d)")).then_inc(s_hst[q], 16)
            pairs(sp, store_h, last=LB)
            sp.wait_ge(s_scat[0], 16 * GR * ((NS + 1) // 2))
            sp.wait_ge(s_scat[1], 16 * GR * (NS // 2))

            sp.wait_ge(s_nov, 1)
            with sp.If(sp.value_load(nov[0:1, 0:1], min_val=0, max_val=OV) > 0):
                sp.dma_start(recov[:, :], rec_dram[bass.ds(OV0, CC), :].rearrange("k (j w) -> (k j) w", w=2)).then_inc(s_ovrec, 16)
                with sp.Fori(1, OV) as j:
                    sp.wait_ge(s_ovadd, j)
                    sp.dma_start(recov[:, :], rec_dram[bass.ds(j * CC + OV0, CC), :].rearrange("k (j w) -> (k j) w", w=2)).then_inc(s_ovrec, 16)

            def load_rec(b, q):
                wait(sp, s_sel, SEL * (b - 1))
                sp.dma_start(recb[:, q, :, :].rearrange("p c w -> p (c w)"),
                             rec_dram[bass.ds(b * CAPC, CAPC), :].rearrange("k w -> (k w)").rearrange("(p n) -> p n", p=P))\
                  .then_inc(s_rec[q], 16)

            def store_out(b, q):
                sp.wait_ge(s_yacc, (NE + 1) * (b + 1))
                sp.dma_start(out[bass.ds(b * BN, BN), :], acc[0:BN, q, :]).then_inc(s_out[q], 16)

            load_rec(0, 0)
            load_rec(1, 1)

            def step(b, q):
                load_rec(b, q)
                if isinstance(b, int) and b - 4 < 0:
                    return
                store_out(b - 4, q)
            step(2, 0)
            step(3, 1)
            pairs(sp, step, first=4)
            for b in range(NB - 4, NB):
                store_out(b, b % 2)
            sp.wait_ge(s_out[0], 16 * ((NB + 1) // 2))
            sp.wait_ge(s_out[1], 16 * (NB // 2))

        @block.gpsimd
        def _(pool):
            pool.memset(dst_i[:, :], 0).then_inc(s_ms, 1)
            pool.memset(ew[:, :], 0.0).then_inc(s_ms, 1)
            pool.memset(src_i[:, :], N).then_inc(s_ms, 1)
            pool.memset(xt[:, LB - 1, :], 0.0).then_inc(s_ms, 1)
            pool.memset(xpb[:, :, :], 0.0).then_inc(s_ms, 1)
            pool.memset(ident[:, :], 0.0).then_inc(s_pool0, 1)
            pool.memset(ones[:, :], 1.0).then_inc(s_pool0, 1)
            pool.memset(zero, 0.0).then_inc(s_pool0, 1)
            pool.iota(iota_row[:, :], pattern=[[1, P]], base=0, channel_multiplier=0,
                      allow_small_or_imprecise_dtypes=True).then_inc(s_pool0, 1)
            pool.iota(ovnum[:, :], pattern=[[1, OV]], base=0, channel_multiplier=0,
                      allow_small_or_imprecise_dtypes=True).then_inc(s_pool0, 1)
            pool.iota(iota_h[:, :], pattern=[[1, P]], base=0, channel_multiplier=0,
                      allow_small_or_imprecise_dtypes=True).then_inc(s_pool0, 1)
            pool.iota(cellnum[:, :, :], pattern=[[0, NS], [P, GR]], base=0, channel_multiplier=1,
                      allow_small_or_imprecise_dtypes=True).then_inc(s_pool0, 1)
            pool.iota(dump0[:, :], pattern=[[SLOTC, NS]], base=DUMP, channel_multiplier=0,
                      allow_small_or_imprecise_dtypes=True).then_inc(s_pool0, 1)
            pool.wait_ge(s_pool0, 8)
            pool.affine_select(out=ident[:, :], in_=ident[:, :], compare_op=ALU.not_equal, fill=1.0,
                               base=0, pattern=[[-1, P]], channel_multiplier=1).then_inc(s_const, 1)
            pool.affine_select(out=lower[:, :], in_=ones[:, :], compare_op=ALU.is_gt, fill=0.0,
                               base=0, pattern=[[1, P]], channel_multiplier=-1).then_inc(s_const, 1)
            pool.dma_start(rec_dram[0:DUMP, :].rearrange("k w -> (k w)").rearrange("(p n) -> p n", p=P), zero).then_inc(s_zero, 16)
            pool.wait_ge(s_zero, 16)
            pool.wait_ge(s_slots, 1)

            def scatter(s, q, g):
                if g == 0:
                    pool.wait_ge(s_cells, 2 * (s + 1))
                    apart(pool)
                pool.indirect_dma_start(rec_dram[:, :], bass.IndirectOffsetOnAxis(ap=placeof[:, q, g:g + 1], axis=0),
                                        cellrow[:, q, g, :, :].rearrange("p j w -> p (j w)"), None).then_inc(s_scat[q], 16)

            def pack_span(s, q):
                for i in range(BT):
                    n = s * BT + i
                    pool.wait_ge(s_hieq, n + 1)
                    apart(pool)
                    nc.gpsimd.tensor_tensor(moving[:, i % 2, :, 0, :], hioh[:, i % 2, :, :], packf[:, bass.ds(n * BW, BW)][:, :, None]
                                            .to_broadcast([P, BW, HI]), ALU.mult).then_inc(s_packed, 1)
                    if not isinstance(s, int) or s > 0:
                        scatter(s - 1, 1 - q, i)
            pairs(pool, pack_span, last=NS)
            for g in range(GR):
                scatter(NS - 1, (NS - 1) % 2, g)
            pool.wait_ge(s_hst[0], 16 * ((LB + 1) // 2))
            pool.wait_ge(s_hst[1], 16 * (LB // 2))

            pool.wait_ge(s_split, 1)
            pool.wait_ge(s_nov, 1)
            with pool.If(pool.value_load(nov[0:1, 0:1], min_val=0, max_val=OV) > 0):
                with pool.Fori(0, OV) as j:
                    pool.wait_ge(s_ovidx, j + 1)
                    apart(pool)
                    pool.indirect_dma_start(
                        G[:, 0, :, :].rearrange("p s d -> p (s d)"), None, h_dram[:, :],
                        bass.IndirectOffsetOnAxis(ap=gidx[:, 0, 0:1], axis=0)).then_inc(s_ovG, 16)
                    pool.wait_ge(s_ovmm, j + 1)
                    apart(pool)
                pool.wait_ge(s_ovmm, OV)

            RING = {0: 4, 4: 8, 8: 12, 12: CH}

            def gather(b, q):
                pool.wait_ge(s_gidx, b + 1)
                for c in range(CH):
                    if c in RING:
                        wait(pool, s_mm, CH * (b - 1) + RING[c])
                        apart(pool)
                    pool.indirect_dma_start(
                        G[:, c, :, :].rearrange("p s d -> p (s d)"), None, h_dram[:, :],
                        bass.IndirectOffsetOnAxis(ap=gidx[:, q, c:c + 1], axis=0)).then_inc(s_G[c], 16)
            gather(0, 0)
            pairs(pool, gather, first=1)

        @block.vector
        def _(dve):
            chain = Chain(dve, s_dve)
            v = nc.vector

            def rsqrt_guess(chain, y, var, t):
                chain(v.tensor_scalar(var, var, 1e-5, None, ALU.add))
                chain(v.tensor_single_scalar(t.bitcast(i32), var.bitcast(i32), 1, ALU.arith_shift_right))
                chain(v.tensor_scalar(y.bitcast(i32), t.bitcast(i32), -1.0, 1597463007.0, ALU.mult, ALU.add))

            def newton_steps(chain, y, var, t, n):
                for _ in range(n):
                    chain(v.tensor_tensor(t, y, y, ALU.mult))
                    chain(v.scalar_tensor_tensor(t, t, -0.5, var, ALU.mult, ALU.mult))
                    chain(v.scalar_tensor_tensor(y, t, 1.5, y, ALU.add, ALU.mult))
            RS = 12
            dve.wait_ge(s_edges, 144)
            dve.wait_ge(s_const, 2)
            chain(v.tensor_copy(srcf[:, :], src_i[:, :]))
            chain(v.tensor_scalar(posf[:, :], srcf[:, :], 1.0 / BN, -(BN - 1) / (2.0 * BN), ALU.mult, ALU.add))
            chain(v.tensor_scalar(blk[:, :], posf[:, :], MAGIC, MAGIC, ALU.add, ALU.subtract))
            v.memset(first_col[:, :], 1.0)
            v.tensor_copy(lanef[:, :], dst_i[:, :])
            chain(v.scalar_tensor_tensor(hif[:, :], blk[:, :], -float(BN), srcf[:, :], ALU.mult, ALU.add))
            chain(v.memset(first_col[:, :].rearrange("p (s c) -> p s c", c=SW)[:, :, 0:1], 0.0))
            chain(v.scalar_tensor_tensor(packf[:, :], lanef[:, :], float(P), hif[:, :], ALU.mult, ALU.add))
            for b in range(NB):
                ins = v.tensor_scalar(onehot[:, b, :], blk[:, :], float(b), None, ALU.is_equal)
            chain(ins)
            chain(v.memset(posf[:, :], 0.0))
            for b in range(NB):
                chain(v.tensor_tensor_scan(rank[:, b % 2, :], first_col[:, :], onehot[:, b, :], 0.0, ALU.mult, ALU.add))
                v.copy_predicated(posf[:, :], onehot[:, b, :].bitcast(mybir.dt.int16), rank[:, b % 2, :])
                last = v.tensor_copy(cnt[:, b, :], rank[:, b % 2, :].rearrange("p (s c) -> p s c", c=SW)[:, :, SW - 1])
            last.then_inc(s_cnt, 1)
            v.memset(not_span0[:, :, :], 1.0)
            v.memset(not_block0[:, :, :], 1.0)
            chain(v.memset(basef[:, :], 65536.0))
            v.memset(not_span0[:, :, 0:1], 0.0)
            chain(v.memset(not_block0[:, :, 0:1], 0.0))
            dve.wait_ge(s_base, 1)
            chain(v.tensor_scalar(cells[:, :, :].rearrange("p b s -> p (b s)"), pmisc[:, 256:256 + NB * NS], 1.0 / CELL, 0.5 - 0.5 / CELL,
                                  ALU.mult, ALU.add))
            chain(v.tensor_scalar(cells[:, :, :], cells[:, :, :], MAGIC, MAGIC, ALU.add, ALU.subtract))
            chain(v.tensor_copy(cells_s[:, :, :], cells[:, :, :].rearrange("p b s -> p s b")))
            chain(v.tensor_tensor_scan(upto_b[:, :, :].rearrange("p b s -> p (b s)"), not_span0[:, :, :].rearrange("p b s -> p (b s)"),
                                       cells[:, :, :].rearrange("p b s -> p (b s)"), 0.0, ALU.mult, ALU.add))
            chain(v.tensor_tensor_scan(upto_s[:, :, :].rearrange("p s b -> p (s b)"), not_block0[:, :, :].rearrange("p s b -> p (s b)"),
                                       cells_s[:, :, :].rearrange("p s b -> p (s b)"), 0.0, ALU.mult, ALU.add))
            v.tensor_tensor(first[:, :, 0:NB], upto_s[:, :, :], cells_s[:, :, :], ALU.subtract)
            v.tensor_copy(first[:, :, NB:NB + 1], upto_s[:, :, NB - 1:NB])
            v.tensor_copy(move[:, :, NB], dump0[:, :])
            chain(v.tensor_tensor(move[:, :, 0:NB], upto_b[:, :, :].rearrange("p b s -> p s b"), cells_s[:, :, :], ALU.subtract))
            chain(v.scalar_tensor_tensor(base[:, :, :], first[:, :, 0:NB], float(CELL),
                                         pmisc[:, 0:NB * NS].rearrange("p (b s) -> p s b", s=NS), ALU.mult, ALU.add))
            for b in range(NB):
                chain(v.copy_predicated(basef[:, :].rearrange("p (s c) -> p s c", c=SW),
                                        onehot[:, b, :].bitcast(mybir.dt.int16).rearrange("p (s c) -> p s c", c=SW),
                                        base[:, :, b:b + 1].to_broadcast([P, NS, SW])))
            chain(v.scalar_tensor_tensor(posf[:, :], posf[:, :], -1.0, basef[:, :], ALU.add, ALU.add))
            chain(v.tensor_copy(slot, posf[:, :]))
            v.tensor_scalar(bits[0], slot, 3, P - 1, ALU.arith_shift_right, ALU.bitwise_and)
            v.tensor_scalar(bits[1], slot, 7, 0xFFF8, ALU.arith_shift_right, ALU.bitwise_and)
            chain(v.tensor_single_scalar(bits[2], slot, CELL - 1, ALU.bitwise_and))
            v.tensor_copy(lanef[:, :], bits[0])
            chain(v.tensor_tensor(hif[:, :], bits[1], bits[2], ALU.add))
            chain(v.tensor_tensor(move[:, :, 0:NB], move[:, :, 0:NB], first[:, :, 0:NB], ALU.subtract))
            chain(v.scalar_tensor_tensor(move[:, :, 0:NB], iota_row[:, None, 0:NB].to_broadcast([P, NS, NB]), float(CAPC),
                                         move[:, :, 0:NB], ALU.mult, ALU.add))
            v.tensor_tensor(movestep[:, :, 1:NB + 1], move[:, :, 1:NB + 1], move[:, :, 0:NB], ALU.subtract)
            v.tensor_copy(movestep[:, :, 0:1], move[:, :, 0:1])
            for s in range(NS):
                ins = v.tensor_tensor(at_least[:, s, :, :], cellnum[:, s, :, None].to_broadcast([P, GR, NB + 1]),
                                      first[:, s, None, :].to_broadcast([P, GR, NB + 1]), ALU.is_ge)
            chain(ins)

            def summed(done, out, per_block):
                for s in range(NS):
                    ins = v.tensor_tensor(steps[:, s, :, :], at_least[:, s, :, :], per_block(s)[:, None, :].to_broadcast([P, GR, NB + 1]),
                                          ALU.mult)
                done(ins)
                done(v.tensor_reduce(out, steps, AX.X, ALU.add))
            summed(chain, pick[:, :, :], lambda s: movestep[:, s, :])
            chain(v.tensor_tensor(place[:, :, :], pick[:, :, :], cellnum[:, :, :], ALU.add))
            chain(v.tensor_scalar(total[:, :], upto_b[:, :, NS - 1], float(-CAPC), 0.0, ALU.add, ALU.max))
            chain(v.tensor_scalar(ovc[:, :], total[:, :], 1.0 / CC, 0.5 - 0.5 / CC, ALU.mult, ALU.add))
            chain(v.tensor_scalar(ovc[:, :], ovc[:, :], MAGIC, MAGIC, ALU.add, ALU.subtract))
            chain(v.tensor_tensor_scan(ovend[:, :], ones[:, 0:NB], ovc[:, :], 0.0, ALU.mult, ALU.add))
            v.tensor_copy(nov[:, :], ovend[:, NB - 1:NB]).then_inc(s_nov, 1)
            dve.wait_ge(s_nov, 1)
            with dve.If(dve.value_load(nov[0:1, 0:1], min_val=0, max_val=OV) > 0):
                n = [0]

                def fix(ins):
                    n[0] += 1
                    ins.then_inc(s_fix, 1)
                    dve.wait_ge(s_fix, n[0])
                fix(v.tensor_tensor(delta[:, 0, :], ovend[:, :], ovc[:, :], ALU.subtract))
                fix(v.tensor_scalar(delta[:, 0, :], delta[:, 0, :], float(CC), float(OV0 - CAPC), ALU.mult, ALU.add))
                fix(v.scalar_tensor_tensor(delta[:, 0, :], iota_row[:, 0:NB], float(-CAPC), delta[:, 0, :], ALU.mult, ALU.add))
                v.tensor_copy(deltastep[:, 0:1], delta[:, 0, 0:1])
                v.tensor_scalar(deltastep[:, NB:NB + 1], delta[:, 0, NB - 1:NB], -1.0, None, ALU.mult)
                fix(v.tensor_tensor(deltastep[:, 1:NB], delta[:, 0, 1:NB], delta[:, 0, 0:NB - 1], ALU.subtract))
                fix(v.tensor_reduce(pick[:, :, :], at_least, AX.X, ALU.add))
                fix(v.scalar_tensor_tensor(pick[:, :, :], pick[:, :, :], float(-CAPC), place[:, :, :], ALU.mult, ALU.add))
                summed(fix, behind[:, :, :], lambda s: deltastep[:, :])
                fix(v.scalar_tensor_tensor(pick[:, :, :], pick[:, :, :], 0.0, behind[:, :, :], ALU.is_ge, ALU.mult))
                fix(v.tensor_tensor(place[:, :, :], place[:, :, :], pick[:, :, :], ALU.add))
                fix(v.memset(ovblk[:, :], 0.0))
                for b in range(NB - 1):
                    fix(v.scalar_tensor_tensor(ovblk[:, :], ovnum[:, :], ovend[0:1, b:b + 1], ovblk[:, :], ALU.is_ge, ALU.add))
                fix(v.tensor_copy(ovblk_i[:, :], ovblk[:, :]))
            v.memset(tmp1[:, 1, :], 0.0).then_inc(s_slots, 1)

            def batches(s, q):
                for i in range(BT):
                    n = s * BT + i
                    wait(dve, s_sorted, n - 1)
                    v.tensor_tensor(laneoh[:, i % 2, :, :], iota_row[:, None, :].to_broadcast([P, BW, P]),
                                    lanef[:, bass.ds(n * BW, BW)][:, :, None].to_broadcast([P, BW, P]), ALU.is_equal)
                    v.tensor_tensor(hioh[:, i % 2, :, :], iota_row[:, None, 0:HI].to_broadcast([P, BW, HI]),
                                    hif[:, bass.ds(n * BW, BW)][:, :, None].to_broadcast([P, BW, HI]), ALU.is_equal).then_inc(s_hieq, 1)
                    dve.wait_ge(s_hieq, n + 1)
                    v.tensor_tensor(moving[:, i % 2, :, 1, :], hioh[:, i % 2, :, :],
                                    ew[:, bass.ds(n * BW, BW)][:, :, None].to_broadcast([P, BW, HI]), ALU.mult).then_inc(s_weighed, 1)
            pairs(dve, batches, last=NS)

            dve.wait_ge(s_w, 112)

            def largest(column, tile):
                return v.tensor_reduce(amax[:, column:column + 1], tile, AX.X, ALU.max, apply_absolute_value=True)
            largest(0, gw[:, :, :].rearrange("p c n -> p (c n)"))
            largest(1, w1s.rearrange("p a n -> p (a n)"))
            largest(2, ew[:, :]).then_inc(s_amax, 1)
            dve.wait_ge(s_amaxT, 1)
            chain(v.reduce_max(amaxT[:, :], pmisc[0:3, 0:P], AX.X))
            v.tensor_scalar(amaxd[:, :], ident[0:3, 0:3], amaxT[:, :], None, ALU.mult).then_inc(s_amaxd, 1)
            dve.wait_ge(s_amaxb, 1)
            chain(v.tensor_scalar(pw[:, :], pmisc[:, 0:3], 1e-30, None, ALU.max))
            chain(v.tensor_single_scalar(pw[:, :].bitcast(i32), pw[:, :].bitcast(i32), 0x7F800000, ALU.bitwise_and))
            chain(v.tensor_scalar(ipw[:, :].bitcast(i32), pw[:, :].bitcast(i32), -1.0, float(0x7F000000), ALU.mult, ALU.add))
            v.tensor_scalar(fac[:, 0:1], ipw[:, 0:1], 2.0 ** 6, None, ALU.mult)
            v.tensor_scalar(fac[:, 1:2], ipw[:, 1:2], 2.0 ** 10, None, ALU.mult)
            v.tensor_scalar(fac[:, 2:3], ipw[:, 2:3], 2.0 ** 10, None, ALU.mult)
            v.tensor_scalar(fac[:, 3:4], pw[:, 1:2], 2.0 ** -20, None, ALU.mult)
            chain(v.tensor_scalar(fac[:, 4:5], pw[:, 0:1], pw[:, 2:3], 2.0 ** -16, ALU.mult, ALU.mult))
            v.memset(tmp1[:, 0, :], 0.0).then_inc(s_fac, 1)
            dve.wait_ge(s_hi, 1)
            v.tensor_tensor(w1p[:, 1, :, :, :].rearrange("p e c n -> p (e c) n"), w1s,
                            w1p[:, 0, :, :, :].rearrange("p e c n -> p (e c) n"), ALU.subtract).then_inc(s_split, 1)

            dve.wait_ge(s_x, 32)
            for b in range(LB):
                ins = v.bn_stats(stx[:, b, :], xt[:, b, :])
            chain(ins)
            for b in range(LB):
                ins = v.bn_aggr(mvx[:, b, :], stx[:, b, :])
            chain(ins)
            chain(v.tensor_copy(varx[:, :], mvx[:, :, 1]))
            v.tensor_copy(meanx[:, :], mvx[:, :, 0])
            rsqrt_guess(chain, rsx[:, :], varx[:, :], tmpx[:, :])
            newton_steps(chain, rsx[:, :], varx[:, :], tmpx[:, :], 3)

            def low_rows(b, q):
                dve.wait_ge(s_hc, b + 1)
                v.scalar_tensor_tensor(hs[:, q, 1, :], py[q][:, 0:D], fac[:, 0:1], hs[:, q, 0, :], ALU.mult, ALU.subtract)\
                 .then_inc(s_hlo, 1)

            def norm(b, q):
                if not isinstance(b, int) or b >= 2:
                    low_rows(b - 2, q)
                wait(dve, s_xhT, b - 1)
                v.tensor_scalar(xh[:, q, :], xt[:, b, :], meanx[:, bass.ds(b, 1)], rsx[:, bass.ds(b, 1)], ALU.subtract, ALU.mult)\
                 .then_inc(s_xh, 1)
            pairs(dve, norm, last=LB)
            low_rows(LB - 2, LB % 2)
            low_rows(LB - 1, (LB - 1) % 2)
            dve.wait_ge(s_xpb, 16)
            dve.wait_ge(s_setC, 3)
            v.tensor_tensor(xpb[:, :, :], xpb[:, :, :], gb[:, None, :].to_broadcast([P, NB, D]), ALU.add)\
             .then_inc(s_xpbready, 1)
            dve.wait_ge(s_xpbready, 1)
            with dve.If(dve.value_load(nov[0:1, 0:1], min_val=0, max_val=OV) > 0):
                with dve.Fori(0, OV) as j:
                    dve.wait_ge(s_ovrec, j * 16 + 16)
                    v.tensor_copy(packi[:, 0, 0:1], recov[:, 0:1])
                    v.tensor_scalar(wh[:, 0, 0:1], recov[:, 1:2], fac[:, 2:3], None, ALU.mult).then_inc(s_ovw, 1)
                    dve.wait_ge(s_ovw, j * 3 + 1)
                    v.tensor_single_scalar(gidx[:, 0, 0:1], packi[:, 0, 0:1], 7, ALU.arith_shift_right).then_inc(s_ovidx, 1)
                    v.tensor_copy(wsc[:, 0, 0, 0:1], wh[:, 0, 0:1])
                    v.scalar_tensor_tensor(wsc[:, 0, 1, 0:1], recov[:, 1:2], fac[:, 2:3], wh[:, 0, 0:1], ALU.mult, ALU.subtract)
                    v.tensor_single_scalar(rowi[:, 0, 0:1], packi[:, 0, 0:1], P - 1, ALU.bitwise_and).then_inc(s_ovw, 1)
                    dve.wait_ge(s_ovw, j * 3 + 2)
                    v.tensor_copy(rowf[:, 0, 0:1], rowi[:, 0, 0:1]).then_inc(s_ovw, 1)
                    dve.wait_ge(s_ovw, j * 3 + 3)
                    for s in range(2):
                        v.tensor_scalar(S[:, 0, 0, s, :], iota_h[:, :], rowf[:, 0, 0:1], wsc[:, 0, s, 0:1], ALU.is_equal,
                                        ALU.mult).then_inc(s_ovS, 1)
                    dve.wait_ge(s_ovmm, j + 1)
                    ob = dve.value_load(ovblk_i[0:1, bass.ds(j, 1)], min_val=0, max_val=NB - 1)
                    v.scalar_tensor_tensor(xpb[:, bass.ds(ob, 1), :].rearrange("p a d -> p (a d)"), pmisc[:, 0:D], fac[:, 4:5],
                                           xpb[:, bass.ds(ob, 1), :].rearrange("p a d -> p (a d)"), ALU.mult, ALU.add)\
                     .then_inc(s_ovadd, 1)
                    dve.wait_ge(s_ovadd, j + 1)
                dve.wait_ge(s_ovadd, OV)
            PRE, ROUT = 2 + RS, 8
            sel, prep, rout = Chain(dve, s_sel), Chain(dve, s_prep), Chain(dve, s_rout)

            def take_apart(b, q):
                dve.wait_ge(s_rec[q], (b - q) * 8 + 16)
                sel.base, sel.n = SEL * b, 0
                weight = recb[:, q, :, 1]
                v.tensor_copy(packi[:, q, :], recb[:, q, :, 0])
                sel(v.tensor_scalar(wh[:, q, :], weight, fac[:, 2:3], None, ALU.mult))
                v.tensor_single_scalar(gidx[:, q, :], packi[:, q, :], 7, ALU.arith_shift_right).then_inc(s_gidx, 1)
                sel(v.tensor_single_scalar(rowi[:, q, :], packi[:, q, :], P - 1, ALU.bitwise_and))
                sel(v.tensor_copy(rowf[:, q, :], rowi[:, q, :]))
                v.tensor_copy(wsc[:, q, 0, :], wh[:, q, :])
                sel(v.scalar_tensor_tensor(wsc[:, q, 1, :], weight, fac[:, 2:3], wh[:, q, :], ALU.mult, ALU.subtract))
                assert sel.n == SEL
                wait(dve, s_mm, CH * (b - 1))

            def select(b, q, parts):
                for i in parts:
                    c, s = i // 2, i % 2
                    v.tensor_scalar(S[:, q, c, s, :], iota_h[:, :], rowf[:, q, c:c + 1],
                                    wsc[:, q, s, c:c + 1], ALU.is_equal, ALU.mult).then_inc(s_S, 1)

            def take_sum(b, q):
                dve.wait_ge(s_mm, CH * (b + 1))
                v.scalar_tensor_tensor(x1[:, q, :], pagg[q][:, 0:D], fac[:, 4:5], xpb[:, b, :], ALU.mult, ALU.add)\
                 .then_inc(s_x1, 1)

            def statistics(b, q):
                prep.base, prep.n = PRE * b, 0
                dve.wait_ge(s_x1, b + 1)
                prep(v.bn_stats(st[:, q, :], x1[:, q, :]))
                apart(dve)
                prep(v.bn_aggr(mv[:, q, :], st[:, q, :]))
                rsqrt_guess(prep, rstd[:, q, :], mv[:, q, 1:2], tmp1[:, q, :])

            def newton(b, q, n):
                newton_steps(prep, rstd[:, q, :], mv[:, q, 1:2], tmp1[:, q, :], n)

            def apply_norm(b, q):
                v.tensor_scalar(x2[:, q, :], x1[:, q, :], mv[:, q, 0:1], rstd[:, q, :], ALU.subtract, ALU.mult)\
                 .then_inc(s_x2, 1)
                assert prep.n == PRE

            def residual(b, q):
                rout.base, rout.n = ROUT * b, 0
                dve.wait_ge(s_x2, b + 1)
                wait(dve, s_out[q], (b - q) * 8)
                rout(v.tensor_tensor(acc[:, q, :], x1[:, q, :], x2[:, q, :], ALU.add))

            def probabilities(b, q):
                t = sm[:, q, :]
                dve.wait_ge(s_ex, b + 1)
                rout(v.reciprocal(t[:, 1:2], t[:, 2:3]))
                rout(v.tensor_scalar(t[:, 8:16], t[:, 16:24], t[:, 1:2], None, ALU.mult))
                apart(dve)
                rout(v.max(t[:, 24:32], t[:, 8:16]))
                apart(dve)
                v.max_index(idx8[:, q, :], t[:, 24:32], t[:, 8:16])
                rout(v.tensor_scalar(t[:, 3:4], t[:, 24:25], t[:, 25:26], 1e-12, ALU.add, ALU.max))
                v.tensor_copy(t[:, 4:6], idx8[:, q, 0:2])

            def combine(b, q):
                t = sm[:, q, :]
                rout(v.reciprocal(t[:, 6:7], t[:, 3:4]))
                rout(v.tensor_scalar(t[:, 32:34], t[:, 24:26], t[:, 6:7], None, ALU.mult))
                v.tensor_scalar(t[:, 40:48], iota_row[:, 0:NE], t[:, 4:5], t[:, 32:33], ALU.is_equal, ALU.mult)
                rout(v.tensor_scalar(t[:, 48:56], iota_row[:, 0:NE], t[:, 5:6], t[:, 33:34], ALU.is_equal, ALU.mult))
                v.tensor_tensor(t[:, 56:64], t[:, 40:48], t[:, 48:56], ALU.add).then_inc(s_comb, 1)
                assert rout.n == ROUT, rout.n

            def top_logit(b, q):
                dve.wait_ge(s_lgc, b + 1)
                v.reduce_max(sm[:, q, 0:1], lg[:, q, :], AX.X, negate=True).then_inc(s_mx, 1)

            def low_tokens(b, q):
                dve.wait_ge(s_x2Tc, 2 * (b + 1))
                v.scalar_tensor_tensor(x2p[:, q, 1, :, :].rearrange("p c n -> p (c n)"), x2T[:, q, :, :].rearrange("p c n -> p (c n)"),
                                       1024.0, x2p[:, q, 0, :, :].rearrange("p c n -> p (c n)"), ALU.mult, ALU.subtract)\
                 .then_inc(s_x2lo, 1)

            def add_bias(b, q):
                dve.wait_ge(s_yb, b + 1)
                dve.wait_ge(s_yacc, (NE + 1) * b + 2)
                v.tensor_tensor(acc[:, q, :], acc[:, q, :], pmisc[:, 256:512], ALU.add).then_inc(s_yacc, 1)

            def add_expert(b, q, e):
                dve.wait_ge(s_y, NE * b + e + 1)
                wait(dve, s_yacc, (NE + 1) * b + added(e))
                v.scalar_tensor_tensor(acc[:, q, :], py[e % 2][:, 0:D], sm[:, q, 56 + e:57 + e], acc[:, q, :],
                                       ALU.mult, ALU.add).then_inc(s_yacc, 1)

            take_apart(0, 0)
            select(0, 0, range(2 * CH))

            def turn(b, q, agg, mid, exp):
                ahead = agg and not (isinstance(b, int) and b + 1 == NB)
                todo = iter(range(2 * CH)) if ahead else iter(())

                def select_next(n=1):
                    select(b + 1, 1 - q, [i for _, i in zip(range(n), todo)])
                prep.between = rout.between = select_next
                if mid:
                    take_sum(b - 1, 1 - q)
                if ahead:
                    take_apart(b + 1, 1 - q)
                if mid:
                    statistics(b - 1, 1 - q)
                for e in range(NE):
                    if mid and e in (0, 1, 2):
                        newton(b - 1, 1 - q, 1)
                    if mid and e == 2:
                        apply_norm(b - 1, 1 - q)
                    if mid and e == 3:
                        residual(b - 1, 1 - q)
                    if mid and e == 4:
                        low_tokens(b - 1, 1 - q)
                    if mid and e == 5:
                        top_logit(b - 1, 1 - q)
                    if mid and e == 7:
                        combine(b - 1, 1 - q)
                    if exp:
                        add_expert(b - 2, q, e)
                    if exp and e == 1:
                        add_bias(b - 2, q)
                    if mid and e == 6:
                        probabilities(b - 1, 1 - q)
                    select_next(2)
                select_next(2 * CH)
            turn(0, 0, True, False, False)
            turn(1, 1, True, True, False)
            pairs(dve, lambda b, q: turn(b, q, True, True, True), first=2, last=NB - 1, steady=4)
            turn(NB - 1, (NB - 1) % 2, True, True, True)
            turn(NB, NB % 2, False, True, True)
            turn(NB + 1, (NB + 1) % 2, False, False, True)

        @block.scalar
        def _(act):
            a = nc.scalar
            act.wait_ge(s_setT, 1)
            a.copy(gb[:, :], ptr[:, 256:512]).then_inc(s_setC, 1)
            a.copy(rwT[:, :, :].rearrange("k c e -> k (c e)"), ptr[:, 64:64 + KC * NE]).then_inc(s_setC, 1)
            a.copy(b1T[:, :], ptr[:, 96:96 + NE * KC]).then_inc(s_setC, 1)

            def cells_out(s, q):
                act.wait_ge(s_sorted, BT * (s + 1))
                wait(act, s_scat[q], (s - q) * 8 * GR)
                a.copy(cellrow[:, q, :, :, :].rearrange("p g j w -> p w (g j)"),
                       pagg[q][:, 0:2 * HI].rearrange("p (w n) -> p w n", w=2)).then_inc(s_cells, 1)
                a.copy(placeof[:, q, :], place[:, bass.ds(s, 1), :].rearrange("p a g -> p (a g)")).then_inc(s_cells, 1)
            act.wait_ge(s_slots, 1)
            pairs(act, cells_out, last=NS)

            act.wait_ge(s_fac, 1)
            act.wait_ge(s_zero, 16)
            a.mul(w1s, w1s, fac[:, 1:2]).then_inc(s_scaled, 1)
            act.wait_ge(s_scaled, 1)
            a.copy(w1p[:, 0, :, :, :].rearrange("p e c n -> p (e c) n"), w1s).then_inc(s_hi, 1)

            def h_rows(b, q):
                act.wait_ge(s_xhT, b + 1)
                wait(act, s_hp, b - 1)
                a.copy(xhT[:, q, :, :].rearrange("k c n -> k (c n)"), ph[q][:, 0:KC * P]).then_inc(s_xhTc, 1)
                act.wait_ge(s_hp, b + 1)
                wait(act, s_hst[q], (b - q) * 8)
                a.mul(hs[:, q, 0, :], py[q][:, 0:D], fac[:, 0:1]).then_inc(s_hc, 1)
            pairs(act, h_rows, last=LB)

            def copy_tokens(b, q):
                act.wait_ge(s_x2T, b + 1)
                a.copy(x2T[:, q, :, :].rearrange("k c n -> k (c n)"), ptr[:, 0:KC * P]).then_inc(s_x2Tc, 1)
                a.mul(x2p[:, q, 0, :, :].rearrange("k c n -> k (c n)"), ptr[:, 0:KC * P], 1024.0).then_inc(s_x2Tc, 1)

            def copy_logits(b, q):
                act.wait_ge(s_lg, b + 1)
                a.copy(lg[:, q, :], pmisc[:, 0:NE]).then_inc(s_lgc, 1)

            def exponentials(b, q):
                act.wait_ge(s_mx, b + 1)
                a.activation(sm[:, q, 16:24], lg[:, q, :], ACT.Exp, bias=sm[:, q, 0:1], scale=1.0,
                             accum_out=sm[:, q, 2:3]).then_inc(s_ex, 1)

            def copy_weights(b, q):
                act.wait_ge(s_cT, b + 1)
                a.copy(combT[:, q, :], ptr[0:NE, 256:256 + P]).then_inc(s_cTc, 1)

            def hidden(b, e):
                act.wait_ge(s_h1, NE * b + e + 1)
                wait(act, s_y, NE * b + e - 1)
                for m in range(KC):
                    ins = a.activation(hT[:, e % 2, m, :], ph[e % 2][:, m * P:(m + 1) * P], ACT.Gelu,
                                       bias=b1T[:, e * KC + m:e * KC + m + 1], scale=fac[:, 3:4])
                ins.then_inc(s_gelu, 1)

            def turn(b, q, agg, mid, exp):
                for e in range(NE):
                    if mid and e == 3:
                        copy_tokens(b - 1, 1 - q)
                    if mid and e == 4:
                        copy_logits(b - 1, 1 - q)
                    if exp and e + 2 < NE:
                        hidden(b - 2, e + 2)
                    if exp and e == 0:
                        copy_weights(b - 2, q)
                    if mid and e + 2 >= NE:
                        hidden(b - 1, e + 2 - NE)
                    if mid and e == 5:
                        exponentials(b - 1, 1 - q)
            turns(act, turn)

        @block.tensor
        def _(pe):
            t = nc.tensor
            pe.wait_ge(s_cnt, 1)
            pe.wait_ge(s_const, 2)
            counts = cnt[:, :, :].rearrange("p b s -> p (b s)")
            t.matmul(pmisc[:, 0:NB * NS], lhsT=lower[:, :], rhs=counts, start=True, stop=True)
            t.matmul(pmisc[:, 256:256 + NB * NS], lhsT=ones[:, :], rhs=counts, start=True, stop=True).then_inc(s_base, 1)
            pe.wait_ge(s_w, 112)
            t.matmul(ptr[:, 256:512], lhsT=ones[0:1, :], rhs=gb_row[:, :], start=True, stop=True)
            for c in range(KC):
                t.transpose(ptr[:, 64 + c * NE:64 + (c + 1) * NE], rw_n[:, c * P:(c + 1) * P], ident[0:NE, 0:NE])
            t.transpose(ptr[:, 96:96 + NE * KC], b1n[:, :], ident[0:NE * KC, 0:NE * KC]).then_inc(s_setT, 1)

            def sort(s, q):
                wait(pe, s_cells, 2 * (s - 1))
                for i in range(BT):
                    n = s * BT + i
                    pe.wait_ge(s_weighed, n + 1)
                    pe.wait_ge(s_packed, n + 1)
                    for c in range(BW):
                        ins = t.matmul(pagg[q][:, 0:2 * HI], lhsT=laneoh[:, i % 2, c, :],
                                       rhs=moving[:, i % 2, c, :, :].rearrange("p w n -> p (w n)"),
                                       start=(i == 0 and c == 0), stop=(i == BT - 1 and c == BW - 1))
                    ins.then_inc(s_sorted, 1)
            pairs(pe, sort, last=NS)

            pe.wait_ge(s_amax, 1)
            t.transpose(pmisc[0:3, 0:P], amax[:, :], ident[:, :]).then_inc(s_amaxT, 1)
            pe.wait_ge(s_amaxd, 1)
            t.matmul(pmisc[:, 0:3], lhsT=ones[0:3, :], rhs=amaxd[:, :], start=True, stop=True).then_inc(s_amaxb, 1)

            def h_rows(b, q):
                pe.wait_ge(s_xh, b + 1)
                wait(pe, s_xhTc, b - 1)
                for c in range(KC):
                    ins = t.transpose(ph[q][:, c * P:(c + 1) * P], xh[:, q, c * P:(c + 1) * P], ident[:, :])
                ins.then_inc(s_xhT, 1)
                pe.wait_ge(s_xhTc, b + 1)
                wait(pe, s_hlo, b - 1)
                for c in range(KC):
                    ins = t.matmul(py[q][:, 0:D], lhsT=xhT[:, q, c, :], rhs=gw[:, c, :], start=(c == 0), stop=(c == KC - 1))
                ins.then_inc(s_hp, 1)
            pairs(pe, h_rows, last=LB)

            PARTS = ((0, 0), (0, 1), (1, 0))

            def sum_rows(psum, weights, rows, first, last):
                for n, (s, r) in enumerate(PARTS):
                    ins = t.matmul(psum, lhsT=weights[:, s, :], rhs=rows[:, r, :], start=(first and n == 0),
                                   stop=(last and n == len(PARTS) - 1))
                return ins

            def aggregate(b, q, chunks):
                for c in chunks:
                    if c == 0:
                        wait(pe, s_x1, b - 1)
                    pe.wait_ge(s_S, 2 * (CH * b + c + 1))
                    pe.wait_ge(s_G[c], (b + 1) * 16)
                    sum_rows(pagg[q][:, 0:D], S[:, q, c, :, :], G[:, c, :, :], c == 0, c == CH - 1).then_inc(s_mm, 1)

            def transpose_tokens(b, q):
                pe.wait_ge(s_x2, b + 1)
                wait(pe, s_cTc, b)
                for c in range(KC):
                    ins = t.transpose(ptr[:, c * P:(c + 1) * P], x2[:, q, c * P:(c + 1) * P], ident[:, :])
                ins.then_inc(s_x2T, 1)

            def logits(b, q):
                pe.wait_ge(s_x2Tc, b * 2 + 1)
                wait(pe, s_yacc, (NE + 1) * (b - 1) + 3)
                for c in range(KC):
                    ins = t.matmul(pmisc[:, 0:NE], lhsT=x2T[:, q, c, :], rhs=rwT[:, c, :], start=(c == 0), stop=(c == KC - 1))
                ins.then_inc(s_lg, 1)

            def transpose_weights(b, q):
                pe.wait_ge(s_comb, b + 1)
                t.transpose(ptr[0:NE, 256:256 + P], sm[:, q, 56:56 + NE], ident[:, :]).then_inc(s_cT, 1)

            def bias(b, q):
                pe.wait_ge(s_cTc, b + 1)
                t.matmul(pmisc[:, 256:512], lhsT=combT[:, q, :], rhs=b2s[:, :], start=True, stop=True).then_inc(s_yb, 1)

            def up(b, q, e):
                if e == 0:
                    pe.wait_ge(s_x2lo, b + 1)
                wait(pe, s_gelu, NE * b + e - 1)
                for m in range(KC):
                    n = 0
                    for c in range(KC):
                        for w, r in PARTS:
                            n += 1
                            ins = t.matmul(ph[e % 2][:, m * P:(m + 1) * P], lhsT=w1p[:, w, e, c, m * P:(m + 1) * P],
                                           rhs=x2p[:, q, r, c, :], start=(n == 1), stop=(n == KC * len(PARTS)))
                ins.then_inc(s_h1, 1)

            def down(b, q, e):
                pe.wait_ge(s_gelu, NE * b + e + 1)
                wait(pe, s_yacc, (NE + 1) * b + (added(e - 2) + 1 if e >= 2 else e - 1))
                for m in range(KC):
                    ins = t.matmul(py[e % 2][:, 0:D], lhsT=hT[:, e % 2, m, :], rhs=w2s[:, e * KC + m, :],
                                   start=(m == 0), stop=(m == KC - 1))
                ins.then_inc(s_y, 1)

            pe.wait_ge(s_xpbready, 1)
            pe.wait_ge(s_split, 1)
            pe.wait_ge(s_nov, 1)
            with pe.If(pe.value_load(nov[0:1, 0:1], min_val=0, max_val=OV) > 0):
                with pe.Fori(0, OV) as j:
                    pe.wait_ge(s_ovS, j * 2 + 2)
                    pe.wait_ge(s_ovG, j * 16 + 16)
                    sum_rows(pmisc[:, 0:D], S[:, 0, 0, :, :], G[:, 0, :, :], True, True).then_inc(s_ovmm, 1)
                    pe.wait_ge(s_ovadd, j + 1)
                pe.wait_ge(s_ovadd, OV)

            def turn(b, q, agg, mid, exp):
                for e in range(NE):
                    if agg:
                        aggregate(b, q, range(CH * e // NE, CH * (e + 1) // NE))
                    if mid and e == 3:
                        transpose_tokens(b - 1, 1 - q)
                    if mid and e == 4:
                        logits(b - 1, 1 - q)
                    if exp and e == 0:
                        transpose_weights(b - 2, q)
                    if exp and e == 1:
                        bias(b - 2, q)
                    if exp:
                        down(b - 2, q, e)
                    if exp and e + 2 < NE:
                        up(b - 2, q, e + 2)
                    if mid and e + 2 >= NE:
                        up(b - 1, 1 - q, e + 2 - NE)
            turns(pe, turn)


INPUTS = ["x", "src", "dst", "edge_weight", "L0_gnn_weight", "L0_gnn_b", "L0_ffn_router_w",
          "L0_ffn_w1", "L0_ffn_b1", "L0_ffn_w2", "L0_ffn_b2"]


def kernel(**inputs):
    import numpy as _np
    import concourse.bacc as _bacc
    from concourse import mybir as _mybir
    from concourse.bass_utils import run_bass_kernel_spmd as _run

    nc = _bacc.Bacc("TRN2", target_bir_lowering=False, num_devices=1)
    arrays, args = {}, []
    for name in INPUTS:
        a = _np.ascontiguousarray(inputs[name])
        arrays[f"in_{name}"] = a
        args.append(nc.dram_tensor(f"in_{name}", a.shape, _mybir.dt.from_np(a.dtype), kind="ExternalInput").ap())
    fp32 = _mybir.dt.float32
    out = nc.dram_tensor("out_0", (3125, 256), fp32, kind="ExternalOutput").ap()
    spans, cap, beyond, slots = room(arrays["in_src"].shape[0])
    cells = (BLOCKS * cap + beyond * 128) // CELL + spans * slots
    rec = nc.dram_tensor("rec_scratch", (cells, 2 * CELL), fp32, kind="Internal").ap()
    h = nc.dram_tensor("h_scratch", (3200, 512), _mybir.dt.float16, kind="Internal").ap()
    build_gnn_moe(nc, *args, out, rec, h)
    r = _run(nc, [arrays], core_ids=[0])
    return r.results[0]["out_0"]
```

```python
import concourse.bass as bass
from concourse import mybir
from contextlib import ExitStack


BLOCKS = 25
CHUNKS = 17
SPAN = 56
CELL = 8


def room(edges):
    spans = -(-edges // (SPAN * 128))
    cap = CHUNKS * 128
    cells = (edges + spans * BLOCKS * (CELL - 1)) // CELL - cap // CELL
    return spans, cap, -(-cells * CELL // 128) + BLOCKS - 1, 1024


def build_gnn_moe(nc, x, src, dst, edge_weight, gnn_w, gnn_b, router_w, w1, b1, w2, b2,
                  out, rec_dram, h_dram):
    fp32 = mybir.dt.float32
    i32 = mybir.dt.int32
    u32 = mybir.dt.uint32
    f16 = mybir.dt.float16
    ALU = mybir.AluOpType
    ACT = mybir.ActivationFunctionType
    AX = mybir.AxisListType

    P = 128
    N, D = x.shape
    E = src.shape[0]
    NS, CAP, OV, SLOTC = room(E)
    NE = router_w.shape[0]
    KC = D // P
    NB = BLOCKS
    BN = N // NB
    SW = SPAN
    EC = NS * SW
    GR = SLOTC // P
    HI = GR * CELL
    BW = 7
    BT = SW // BW
    HS = BT // 2
    CH = CAP // P
    CAPC = CAP // CELL
    CC = P // CELL
    OV0 = NB * CAPC
    DUMP = OV0 + OV * CC
    CWORDS = 2 * CELL
    LB = -(-N // P)
    LR = N - (LB - 1) * P
    MAGIC = 12582912.0

    with ExitStack() as ctx:
        def sb(name, shape, dt=fp32):
            return ctx.enter_context(nc.sbuf_tensor(name, shape, dt))

        def pb(name, shape, dt=fp32):
            return ctx.enter_context(nc.psum_tensor(name, shape, dt))

        def sem(name):
            return ctx.enter_context(nc.semaphore(name))

        ident = sb("ident", [P, P])
        lower = sb("lower", [P, P])
        ones = sb("ones", [P, P])
        iota_row = sb("iota_row", [P, P])
        src_i = sb("src_i", [P, EC], i32)
        dst_i = sb("dst_i", [P, EC], i32)
        ew = sb("ew", [P, EC])
        srcf = sb("srcf", [P, EC])
        blk = sb("blk", [P, EC])
        onehot = sb("onehot", [P, NB, EC], f16)
        first_col = sb("first_col", [P, EC])
        rank = sb("rank", [P, 2, EC])
        posf = sb("posf", [P, EC])
        basef = sb("basef", [P, EC])
        slot = src_i[:, :]
        bits = [dst_i[:, :], rank[:, 0, :].bitcast(i32), rank[:, 1, :].bitcast(i32)]
        lanef = sb("lanef", [P, EC])
        hif = sb("hif", [P, EC])
        packf = sb("packf", [P, EC])
        cnt = sb("cnt", [P, NB, NS])
        cells = sb("cells", [P, NB, NS])
        cells_s = sb("cells_s", [P, NS, NB])
        not_span0 = sb("not_span0", [P, NB, NS])
        not_block0 = sb("not_block0", [P, NS, NB])
        upto_b = sb("upto_b", [P, NB, NS])
        upto_s = sb("upto_s", [P, NS, NB])
        first = sb("first", [P, NS, NB + 1])
        move = sb("move", [P, NS, NB + 1])
        movestep = sb("movestep", [P, NS, NB + 1])
        base = sb("base", [P, NS, NB])
        cellnum = sb("cellnum", [P, NS, GR])
        dump0 = sb("dump0", [P, NS])
        place = sb("place", [P, NS, GR])
        pick = sb("pick", [P, NS, GR])
        cellrow = sb("cellrow", [P, 2, GR, CELL, 2])
        placeof = sb("placeof", [P, 2, GR], i32)
        total = sb("total", [P, NB])
        ovc = sb("ovc", [P, NB])
        ovend = sb("ovend", [P, NB])
        behind = sb("behind", [P, NS, GR])
        deltastep = sb("deltastep", [P, NB + 1])
        delta = sb("delta", [P, 1, NB])
        nov = sb("nov", [P, 1], i32)
        ovblk = sb("ovblk", [1, OV])
        ovblk_i = sb("ovblk_i", [1, OV], i32)
        ovnum = sb("ovnum", [1, OV])
        recov = sb("recov", [P, 2])

        xt = sb("xt", [P, LB, D])
        xpb = sb("xpb", [P, NB, D])
        gw = sb("gw", [P, KC, D])
        gb_row = sb("gb_row", [1, D])
        gb = sb("gb", [P, D])
        rw_n = sb("rw_n", [NE, D])
        rwT = sb("rwT", [P, KC, NE])
        w1p = sb("w1p", [P, 2, NE, KC, D], f16)
        w2s = sb("w2s", [P, NE * KC, D])
        amax = sb("amax", [P, 3])
        amaxT = sb("amaxT", [3, 1])
        amaxd = sb("amaxd", [3, 3])
        pw = sb("pw", [P, 3])
        ipw = sb("ipw", [P, 3])
        fac = sb("fac", [P, 5])
        b1n = sb("b1n", [NE * KC, P])
        b1T = sb("b1T", [P, NE * KC])
        b2s = sb("b2s", [NE, D])

        st = sb("st", [P, 2, 6])
        mv = sb("mv", [P, 2, 2])
        rstd = sb("rstd", [P, 2, 1])
        tmp1 = sb("tmp1", [P, 2, 1])
        sumx = sb("sumx", [P, LB])
        varx = sb("varx", [P, LB])
        minus_mean = sb("minus_mean", [P, LB])
        shiftx = sb("shiftx", [P, LB])
        rsx = sb("rsx", [P, LB])
        tmpx = sb("tmpx", [P, LB])
        xh = sb("xh", [P, 2, D])
        xhT = sb("xhT", [P, 2, KC, P])
        hs = sb("hs", [P, 2, 2, D], f16)

        recb = sb("recb", [P, 2, CH, 2])
        packi = sb("packi", [P, 2, CH], i32)
        gidx = sb("gidx", [P, 2, CH], i32)
        rowi = sb("rowi", [P, 2, CH], i32)
        rowf = sb("rowf", [P, 2, CH])
        S = sb("S", [P, 2, CH, 2, P], f16)
        G = sb("G", [P, CH, 2, D], f16)
        w1s = G[:, :, :, :].rearrange("p c s d -> p (c s d)").bitcast(fp32)[:, 0:NE * KC * D]\
            .rearrange("p (a n) -> p a n", n=D)
        sort_room = S[:, :, :, :, :].rearrange("p a c s n -> p (a c s n)").bitcast(fp32)
        laneoh = sort_room[:, 0:2 * BW * P].rearrange("p (a c n) -> p a c n", a=2, n=P)
        moving = sort_room[:, 2 * BW * P:2 * BW * (P + 2 * HI)].rearrange("p (a c w n) -> p a c w n", a=2, w=2, n=HI)
        hioh = sb("hioh", [P, 2, BW, HI])
        at_least = sort_room[:, 0:NS * GR * (NB + 1)].rearrange("p (s g b) -> p s g b", s=NS, g=GR)
        steps = sort_room[:, NS * GR * (NB + 1):2 * NS * GR * (NB + 1)].rearrange("p (s g b) -> p s g b", s=NS, g=GR)
        zero = w1p[:, :, :, :, :].rearrange("p s e c n -> p (s e c n)").bitcast(fp32)[:, 0:DUMP * CWORDS // P]
        iota_h = sb("iota_h", [P, P], f16)
        wsc = sb("wsc", [P, 2, 3, CH])
        wh = sb("wh", [P, 2, CH], f16)
        x1 = sb("x1", [P, 2, D])
        x2 = sb("x2", [P, 2, D])
        x2T = sb("x2T", [P, 2, KC, P])
        x2p = sb("x2p", [P, 2, 2, KC, P], f16)
        acc = sb("acc", [P, 2, D])
        hT = sb("hT", [P, 2, KC, P])
        sm = sb("sm", [P, 2, 64])
        lg = sb("lg", [P, 2, NE])
        idx8 = sb("idx8", [P, 2, 8], u32)
        combT = sb("combT", [NE, 2, P])

        pagg = [pb(f"pagg{i}", [P, 512]) for i in range(2)]
        ptr = pb("ptr", [P, 512])
        pmisc = pb("pmisc", [P, 512])
        ph = [pb(f"ph{i}", [P, 512]) for i in range(2)]
        py = [pb(f"py{i}", [P, 512]) for i in range(2)]

        s_turn = sem("s_turn")
        s_fix = sem("s_fix")
        s_src = sem("s_src")
        s_edges = sem("s_edges")
        s_blk = sem("s_blk")
        s_onehot = sem("s_onehot")
        s_x = sem("s_x")
        s_xpb = sem("s_xpb")
        s_w = sem("s_w")
        s_pool0 = sem("s_pool0")
        s_const = sem("s_const")
        s_ms = sem("s_ms")
        s_zero = sem("s_zero")
        s_dve = sem("s_dve")
        s_rank = sem("s_rank")
        s_taken = sem("s_taken")
        s_base = sem("s_base")
        s_slots = sem("s_slots")
        s_hieq = sem("s_hieq")
        s_weighed = sem("s_weighed")
        s_packed = sem("s_packed")
        s_sorted = sem("s_sorted")
        s_cells = sem("s_cells")
        s_scat = [sem(f"s_scat{i}") for i in range(2)]
        s_gidx = sem("s_gidx")
        s_ovidx = sem("s_ovidx")
        s_setT = sem("s_setT")
        s_setC = sem("s_setC")
        s_xh = sem("s_xh")
        s_sumx = sem("s_sumx")
        s_varx = sem("s_varx")
        s_xnorm = sem("s_xnorm")
        s_xhT = sem("s_xhT")
        s_xhTc = sem("s_xhTc")
        s_hp = sem("s_hp")
        s_hc = sem("s_hc")
        s_hst = [sem(f"s_hst{i}") for i in range(2)]
        s_xpbready = sem("s_xpbready")

        s_nov = sem("s_nov")
        s_sel = sem("s_sel")
        s_prep = sem("s_prep")
        s_rout = sem("s_rout")
        s_amax = sem("s_amax")
        s_amaxT = sem("s_amaxT")
        s_amaxd = sem("s_amaxd")
        s_amaxb = sem("s_amaxb")
        s_fac = sem("s_fac")
        s_scaled = sem("s_scaled")
        s_hi = sem("s_hi")
        s_split = sem("s_split")
        s_hlo = sem("s_hlo")
        s_ovw = sem("s_ovw")
        s_x2lo = sem("s_x2lo")
        s_ovrec = sem("s_ovrec")
        s_ovS = sem("s_ovS")
        s_ovG = sem("s_ovG")
        s_ovmm = sem("s_ovmm")
        s_ovadd = sem("s_ovadd")
        s_rec = [sem(f"s_rec{i}") for i in range(2)]
        s_G = [sem(f"s_G{i}") for i in range(CH)]
        s_S = sem("s_S")
        s_mm = sem("s_mm")
        s_x1 = sem("s_x1")
        s_x2 = sem("s_x2")
        s_x2T = sem("s_x2T")
        s_x2Tc = sem("s_x2Tc")
        s_lg = sem("s_lg")
        s_mx = sem("s_mx")
        s_lgc = sem("s_lgc")
        s_ex = sem("s_ex")
        s_comb = sem("s_comb")
        s_cT = sem("s_cT")
        s_cTc = sem("s_cTc")
        s_yb = sem("s_yb")
        s_h1 = sem("s_h1")
        s_gelu = sem("s_gelu")
        s_y = sem("s_y")
        s_yacc = sem("s_yacc")
        s_out = [sem(f"s_out{i}") for i in range(2)]

        block = ctx.enter_context(nc.Block())

        def pairs(eng, body, first=0, last=NB, steady=2):
            b = first
            while b < steady or b % 2:
                body(b, b % 2)
                b += 1
            turns = (last - b) // 2
            if turns:
                with eng.Fori(0, turns) as i:
                    body(i * 2 + b, 0)
                    body(i * 2 + (b + 1), 1)
            b += 2 * turns
            if b < last:
                body(b, 0)

        def added(e):
            return e if e < 3 else e + 1

        def apart(eng):
            eng.sem_inc(s_turn, 1)

        def wait(eng, s, n):
            if not isinstance(n, int) or n > 0:
                eng.wait_ge(s, n)

        def turns(eng, turn):
            turn(0, 0, True, False, False)
            turn(1, 1, True, True, False)
            pairs(eng, lambda b, q: turn(b, q, True, True, True), first=2, steady=4)
            turn(NB, NB % 2, False, True, True)
            turn(NB + 1, (NB + 1) % 2, False, False, True)

        SEL = 4

        def beside(s):
            return range(min(HS, LB - s * HS)) if isinstance(s, int) else range(HS)

        class Chain:
            def __init__(self, eng, done):
                self.eng, self.done, self.base, self.n = eng, done, 0, 0
                self.between = None

            def __call__(self, ins):
                self.n += 1
                ins.then_inc(self.done, 1)
                if self.between:
                    self.between()
                self.eng.wait_ge(self.done, self.base + self.n)

        @block.sync
        def _(sp):
            full = (NS - 1) * P * SW
            rows = (E - full) // SW
            rest = E - full - rows * SW
            sp.wait_ge(s_ms, 3)
            for tile, dram in ((src_i, src), (dst_i, dst), (ew, edge_weight)):
                loaded = s_src if tile is src_i else s_edges
                by_span = tile[:, :].rearrange("p (s c) -> p s c", c=SW)
                sp.dma_start(by_span[:, 0:NS - 1, :], dram[0:full].rearrange("(s p c) -> p s c", p=P, c=SW)).then_inc(loaded, 16)
                sp.dma_start(by_span[0:rows, NS - 1, :], dram[full:full + rows * SW].rearrange("(p c) -> p c", c=SW)).then_inc(loaded, 16)
                sp.dma_start(by_span[rows:rows + 1, NS - 1, 0:rest], dram[full + rows * SW:E].rearrange("(p c) -> p c", p=1))\
                  .then_inc(loaded, 16)
            sp.wait_ge(s_ms, 4)
            sp.dma_start(xt[:, 0:LB - 1, :], x[0:(LB - 1) * P, :].rearrange("(b p) d -> p b d", p=P)).then_inc(s_x, 16)
            sp.dma_start(xt[0:LR, LB - 1, :], x[(LB - 1) * P:N, :]).then_inc(s_x, 16)
            sp.dma_start(gw[:, :, :], gnn_w.rearrange("(c k) n -> k c n", k=P)).then_inc(s_w, 16)
            sp.dma_start(gb_row[:, :], gnn_b.rearrange("(a n) -> a n", a=1)).then_inc(s_w, 16)
            sp.dma_start(rw_n[:, :], router_w).then_inc(s_w, 16)
            sp.dma_start(b1n[:, :], b1.rearrange("e (c k) -> (e c) k", k=P)).then_inc(s_w, 16)
            sp.dma_start(b2s[:, :], b2).then_inc(s_w, 16)
            sp.dma_start(w1s, w1.rearrange("e (c k) n -> k (e c) n", k=P)).then_inc(s_w, 16)
            sp.dma_start(w2s[:, :, :], w2.rearrange("e (c k) n -> k (e c) n", k=P)).then_inc(s_w, 16)
            sp.wait_ge(s_ms, 5)
            sp.dma_start(xpb[0:BN, :, :], x.rearrange("(b p) d -> p b d", p=BN)).then_inc(s_xpb, 16)

            def store_h(b, q):
                sp.wait_ge(s_hlo, b + 1)
                sp.dma_start(h_dram[bass.ds(b * P, P), :], hs[:, q, :, :].rearrange("p s d -> p (s d)")).then_inc(s_hst[q], 16)
            pairs(sp, store_h, last=LB)
            sp.wait_ge(s_scat[0], 16 * GR * ((NS + 1) // 2))
            sp.wait_ge(s_scat[1], 16 * GR * (NS // 2))

            sp.wait_ge(s_nov, 1)
            with sp.If(sp.value_load(nov[0:1, 0:1], min_val=0, max_val=OV) > 0):
                sp.dma_start(recov[:, :], rec_dram[bass.ds(OV0, CC), :].rearrange("k (j w) -> (k j) w", w=2)).then_inc(s_ovrec, 16)
                with sp.Fori(1, OV) as j:
                    sp.wait_ge(s_ovadd, j)
                    sp.dma_start(recov[:, :], rec_dram[bass.ds(j * CC + OV0, CC), :].rearrange("k (j w) -> (k j) w", w=2)).then_inc(s_ovrec, 16)

            def load_rec(b, q):
                wait(sp, s_sel, SEL * (b - 1))
                sp.dma_start(recb[:, q, :, :].rearrange("p c w -> p (c w)"),
                             rec_dram[bass.ds(b * CAPC, CAPC), :].rearrange("k w -> (k w)").rearrange("(p n) -> p n", p=P))\
                  .then_inc(s_rec[q], 16)

            def store_out(b, q):
                sp.wait_ge(s_yacc, (NE + 1) * (b + 1))
                sp.dma_start(out[bass.ds(b * BN, BN), :], acc[0:BN, q, :]).then_inc(s_out[q], 16)

            load_rec(0, 0)
            load_rec(1, 1)

            load_rec(2, 0)
            load_rec(3, 1)

            def step(b, q):
                load_rec(b, q)
                store_out(b - 4, q)
            pairs(sp, step, first=4)
            for b in range(NB - 4, NB):
                store_out(b, b % 2)
            sp.wait_ge(s_out[0], 16 * ((NB + 1) // 2))
            sp.wait_ge(s_out[1], 16 * (NB // 2))

        @block.gpsimd
        def _(pool):
            pool.memset(dst_i[:, :], 0).then_inc(s_ms, 1)
            pool.memset(ew[:, :], 0.0).then_inc(s_ms, 1)
            pool.memset(src_i[:, :], N).then_inc(s_ms, 1)
            pool.memset(xt[:, LB - 1, :], 0.0).then_inc(s_ms, 1)
            pool.memset(ident[:, :], 0.0).then_inc(s_pool0, 1)
            pool.memset(ones[:, :], 1.0).then_inc(s_pool0, 1)
            pool.memset(zero, 0.0).then_inc(s_pool0, 1)
            pool.iota(iota_row[:, :], pattern=[[1, P]], base=0, channel_multiplier=0,
                      allow_small_or_imprecise_dtypes=True).then_inc(s_pool0, 1)
            pool.iota(ovnum[:, :], pattern=[[1, OV]], base=0, channel_multiplier=0,
                      allow_small_or_imprecise_dtypes=True).then_inc(s_pool0, 1)
            pool.iota(iota_h[:, :], pattern=[[1, P]], base=0, channel_multiplier=0,
                      allow_small_or_imprecise_dtypes=True).then_inc(s_pool0, 1)
            pool.iota(cellnum[:, :, :], pattern=[[0, NS], [P, GR]], base=0, channel_multiplier=1,
                      allow_small_or_imprecise_dtypes=True).then_inc(s_pool0, 1)
            pool.iota(dump0[:, :], pattern=[[SLOTC, NS]], base=DUMP, channel_multiplier=0,
                      allow_small_or_imprecise_dtypes=True).then_inc(s_pool0, 1)
            pool.wait_ge(s_pool0, 8)
            pool.affine_select(out=ident[:, :], in_=ident[:, :], compare_op=ALU.not_equal, fill=1.0,
                               base=0, pattern=[[-1, P]], channel_multiplier=1).then_inc(s_const, 1)
            pool.affine_select(out=lower[:, :], in_=ones[:, :], compare_op=ALU.is_gt, fill=0.0,
                               base=0, pattern=[[1, P]], channel_multiplier=-1).then_inc(s_const, 1)
            pool.wait_ge(s_blk, 1)
            for b in range(NB):
                nc.gpsimd.tensor_scalar(onehot[:, b, :], blk[:, :], float(b), None, ALU.is_equal).then_inc(s_onehot, 1)
            pool.dma_start(rec_dram[0:DUMP, :].rearrange("k w -> (k w)").rearrange("(p n) -> p n", p=P), zero).then_inc(s_zero, 16)
            pool.memset(xpb[:, :, :], 0.0).then_inc(s_ms, 1)
            pool.wait_ge(s_zero, 16)
            pool.wait_ge(s_xpb, 16)
            pool.wait_ge(s_setC, 1)
            nc.gpsimd.tensor_tensor(xpb[:, :, :], xpb[:, :, :], gb[:, None, :].to_broadcast([P, NB, D]), ALU.add)\
              .then_inc(s_xpbready, 1)
            pool.wait_ge(s_slots, 1)

            def scatter(s, q, g):
                if g == 0:
                    pool.wait_ge(s_cells, 2 * (s + 1))
                    apart(pool)
                pool.indirect_dma_start(rec_dram[:, :], bass.IndirectOffsetOnAxis(ap=placeof[:, q, g:g + 1], axis=0),
                                        cellrow[:, q, g, :, :].rearrange("p j w -> p (j w)"), None).then_inc(s_scat[q], 16)

            LATER = [range(max(i - 1, 0), i if i + 1 < BT else GR) for i in range(BT)]

            def pack_span(s, q):
                for i in range(BT):
                    n = s * BT + i
                    wait(pool, s_sorted, n - 1)
                    pool.wait_ge(s_hieq, n + 1)
                    apart(pool)
                    nc.gpsimd.tensor_tensor(moving[:, i % 2, :, 0, :], hioh[:, i % 2, :, :], packf[:, bass.ds(n * BW, BW)][:, :, None]
                                            .to_broadcast([P, BW, HI]), ALU.mult).then_inc(s_packed, 1)
                    if not isinstance(s, int) or s > 0:
                        for g in LATER[i]:
                            scatter(s - 1, 1 - q, g)
                    if isinstance(s, int) and s == NS - 1:
                        pool.wait_ge(s_hi, 1)
                        for e in range(NE * i // BT, NE * (i + 1) // BT):
                            nc.gpsimd.tensor_tensor(w1p[:, 1, e, :, :], w1s[:, e * KC:(e + 1) * KC, :], w1p[:, 0, e, :, :], ALU.subtract)\
                              .then_inc(s_split, 1)
            pairs(pool, pack_span, last=NS)
            for g in range(GR):
                scatter(NS - 1, (NS - 1) % 2, g)
            pool.wait_ge(s_hst[0], 16 * ((LB + 1) // 2))
            pool.wait_ge(s_hst[1], 16 * (LB // 2))

            pool.wait_ge(s_split, NE)
            pool.wait_ge(s_nov, 1)
            with pool.If(pool.value_load(nov[0:1, 0:1], min_val=0, max_val=OV) > 0):
                with pool.Fori(0, OV) as j:
                    pool.wait_ge(s_ovidx, j + 1)
                    apart(pool)
                    pool.indirect_dma_start(
                        G[:, 0, :, :].rearrange("p s d -> p (s d)"), None, h_dram[:, :],
                        bass.IndirectOffsetOnAxis(ap=gidx[:, 0, 0:1], axis=0)).then_inc(s_ovG, 16)
                    pool.wait_ge(s_ovmm, j + 1)
                    apart(pool)
                pool.wait_ge(s_ovmm, OV)

            RING = {0: 4, 4: 8, 8: 12, 12: CH}

            def gather(b, q):
                pool.wait_ge(s_gidx, b + 1)
                for c in range(CH):
                    if c in RING:
                        wait(pool, s_mm, CH * (b - 1) + RING[c])
                        apart(pool)
                    pool.indirect_dma_start(
                        G[:, c, :, :].rearrange("p s d -> p (s d)"), None, h_dram[:, :],
                        bass.IndirectOffsetOnAxis(ap=gidx[:, q, c:c + 1], axis=0)).then_inc(s_G[c], 16)
            gather(0, 0)
            pairs(pool, gather, first=1)

        @block.vector
        def _(dve):
            chain = Chain(dve, s_dve)
            v = nc.vector

            def rsqrt_guess(chain, y, var, t):
                chain(v.tensor_scalar(var, var, 1e-5, None, ALU.add))
                chain(v.tensor_single_scalar(t.bitcast(i32), var.bitcast(i32), 1, ALU.arith_shift_right))
                chain(v.tensor_scalar(y.bitcast(i32), t.bitcast(i32), -1.0, 1597463007.0, ALU.mult, ALU.add))

            def newton_steps(chain, y, var, t, n):
                for _ in range(n):
                    chain(v.tensor_tensor(t, y, y, ALU.mult))
                    chain(v.scalar_tensor_tensor(t, t, -0.5, var, ALU.mult, ALU.mult))
                    chain(v.scalar_tensor_tensor(y, t, 1.5, y, ALU.add, ALU.mult))
            RS = 12
            v.memset(first_col[:, :], 1.0)
            v.memset(not_span0[:, :, :], 1.0)
            v.memset(not_block0[:, :, :], 1.0)
            v.memset(posf[:, :], 0.0)
            chain(v.memset(basef[:, :], 65536.0))
            v.memset(not_span0[:, :, 0:1], 0.0)
            v.memset(not_block0[:, :, 0:1], 0.0)
            v.memset(first_col[:, :].rearrange("p (s c) -> p s c", c=SW)[:, :, 0:1], 0.0)
            dve.wait_ge(s_src, 48)
            chain(v.tensor_copy(srcf[:, :], src_i[:, :]))
            chain(v.tensor_scalar(hif[:, :], srcf[:, :], 1.0 / BN, -(BN - 1) / (2.0 * BN), ALU.mult, ALU.add))
            v.tensor_scalar(blk[:, :], hif[:, :], MAGIC, MAGIC, ALU.add, ALU.subtract).then_inc(s_blk, 1)
            dve.wait_ge(s_blk, 1)
            chain(v.scalar_tensor_tensor(hif[:, :], blk[:, :], -float(BN), srcf[:, :], ALU.mult, ALU.add))
            dve.wait_ge(s_edges, 96)
            dve.wait_ge(s_const, 2)
            chain(v.tensor_copy(lanef[:, :], dst_i[:, :]))
            chain(v.scalar_tensor_tensor(packf[:, :], lanef[:, :], float(P), hif[:, :], ALU.mult, ALU.add))

            ranks = (rank[:, 0, :], rank[:, 1, :], srcf[:, :])
            def take_ranks(b):
                dve.wait_ge(s_rank, b + 1)
                wait(dve, s_taken, b)
                v.copy_predicated(posf[:, :], onehot[:, b, :].bitcast(mybir.dt.int16), ranks[b % 3])
                v.tensor_copy(cnt[:, b, :], ranks[b % 3].rearrange("p (s c) -> p s c", c=SW)[:, :, SW - 1]).then_inc(s_taken, 1)
            for b in range(NB):
                dve.wait_ge(s_onehot, b + 1)
                wait(dve, s_taken, b - 2)
                v.tensor_tensor_scan(ranks[b % 3], first_col[:, :], onehot[:, b, :], 0.0, ALU.mult, ALU.add).then_inc(s_rank, 1)
                if b > 0:
                    take_ranks(b - 1)
            take_ranks(NB - 1)
            dve.wait_ge(s_w, 112)

            def largest(column, tile):
                return v.tensor_reduce(amax[:, column:column + 1], tile, AX.X, ALU.max, apply_absolute_value=True)
            largest(0, gw[:, :, :].rearrange("p c n -> p (c n)"))
            largest(1, w1s.rearrange("p a n -> p (a n)"))
            largest(2, ew[:, :]).then_inc(s_amax, 1)
            v.memset(not_span0[:, :, 0:1], 0.0)
            chain(v.memset(not_block0[:, :, 0:1], 0.0))
            dve.wait_ge(s_base, 1)
            chain(v.tensor_scalar(cells[:, :, :].rearrange("p b s -> p (b s)"), pmisc[:, 256:256 + NB * NS], 1.0 / CELL, 0.5 - 0.5 / CELL,
                                  ALU.mult, ALU.add))
            chain(v.tensor_scalar(cells[:, :, :], cells[:, :, :], MAGIC, MAGIC, ALU.add, ALU.subtract))
            chain(v.tensor_copy(cells_s[:, :, :], cells[:, :, :].rearrange("p b s -> p s b")))
            chain(v.tensor_tensor_scan(upto_b[:, :, :].rearrange("p b s -> p (b s)"), not_span0[:, :, :].rearrange("p b s -> p (b s)"),
                                       cells[:, :, :].rearrange("p b s -> p (b s)"), 0.0, ALU.mult, ALU.add))
            chain(v.tensor_tensor_scan(upto_s[:, :, :].rearrange("p s b -> p (s b)"), not_block0[:, :, :].rearrange("p s b -> p (s b)"),
                                       cells_s[:, :, :].rearrange("p s b -> p (s b)"), 0.0, ALU.mult, ALU.add))
            v.tensor_tensor(first[:, :, 0:NB], upto_s[:, :, :], cells_s[:, :, :], ALU.subtract)
            v.tensor_copy(first[:, :, NB:NB + 1], upto_s[:, :, NB - 1:NB])
            v.tensor_copy(move[:, :, NB], dump0[:, :])
            chain(v.tensor_tensor(move[:, :, 0:NB], upto_b[:, :, :].rearrange("p b s -> p s b"), cells_s[:, :, :], ALU.subtract))
            chain(v.scalar_tensor_tensor(base[:, :, :], first[:, :, 0:NB], float(CELL),
                                         pmisc[:, 0:NB * NS].rearrange("p (b s) -> p s b", s=NS), ALU.mult, ALU.add))
            def norm_step(k):
                y, var, g = rsx[:, :], varx[:, :], tmpx[:, :]
                if k == 0:
                    dve.wait_ge(s_varx, LB)
                    v.tensor_scalar(var, var, 1.0 / D, 1e-5, ALU.mult, ALU.add)
                elif k == 1:
                    v.tensor_single_scalar(g.bitcast(i32), var.bitcast(i32), 1, ALU.arith_shift_right)
                elif k == 2:
                    v.tensor_scalar(y.bitcast(i32), g.bitcast(i32), -1.0, 1597463007.0, ALU.mult, ALU.add)
                elif k < 12 and k % 3 == 0:
                    v.tensor_tensor(g, y, y, ALU.mult)
                elif k < 12 and k % 3 == 1:
                    v.scalar_tensor_tensor(g, g, -0.5, var, ALU.mult, ALU.mult)
                elif k < 12:
                    v.scalar_tensor_tensor(y, g, 1.5, y, ALU.add, ALU.mult)
                elif k == 12:
                    v.tensor_tensor(shiftx[:, :], minus_mean[:, :], y, ALU.mult).then_inc(s_xnorm, 1)
            for b in range(NB):
                if b < NS:
                    v.tensor_tensor(at_least[:, b, :, :], cellnum[:, b, :, None].to_broadcast([P, GR, NB + 1]),
                                    first[:, b, None, :].to_broadcast([P, GR, NB + 1]), ALU.is_ge)
                else:
                    norm_step(b - NS)
                chain(v.copy_predicated(basef[:, :].rearrange("p (s c) -> p s c", c=SW),
                                        onehot[:, b, :].bitcast(mybir.dt.int16).rearrange("p (s c) -> p s c", c=SW),
                                        base[:, :, b:b + 1].to_broadcast([P, NS, SW])))
            chain(v.scalar_tensor_tensor(posf[:, :], posf[:, :], -1.0, basef[:, :], ALU.add, ALU.add))
            chain(v.tensor_copy(slot, posf[:, :]))
            v.tensor_scalar(bits[0], slot, 3, P - 1, ALU.arith_shift_right, ALU.bitwise_and)
            v.tensor_scalar(bits[1], slot, 7, 0xFFF8, ALU.arith_shift_right, ALU.bitwise_and)
            chain(v.tensor_single_scalar(bits[2], slot, CELL - 1, ALU.bitwise_and))
            v.tensor_copy(lanef[:, :], bits[0])
            chain(v.tensor_tensor(hif[:, :], bits[1], bits[2], ALU.add))
            dve.wait_ge(s_amaxT, 1)
            chain(v.reduce_max(amaxT[:, :], ptr[0:3, 0:P], AX.X))
            v.tensor_scalar(amaxd[:, :], ident[0:3, 0:3], amaxT[:, :], None, ALU.mult).then_inc(s_amaxd, 1)
            chain(v.tensor_tensor(move[:, :, 0:NB], move[:, :, 0:NB], first[:, :, 0:NB], ALU.subtract))
            chain(v.scalar_tensor_tensor(move[:, :, 0:NB], iota_row[:, None, 0:NB].to_broadcast([P, NS, NB]), float(CAPC),
                                         move[:, :, 0:NB], ALU.mult, ALU.add))
            v.tensor_tensor(movestep[:, :, 1:NB + 1], move[:, :, 1:NB + 1], move[:, :, 0:NB], ALU.subtract)
            chain(v.tensor_copy(movestep[:, :, 0:1], move[:, :, 0:1]))

            def summed(done, out, per_block):
                for s in range(NS):
                    ins = v.tensor_tensor(steps[:, s, :, :], at_least[:, s, :, :], per_block(s)[:, None, :].to_broadcast([P, GR, NB + 1]),
                                          ALU.mult)
                done(ins)
                done(v.tensor_reduce(out, steps, AX.X, ALU.add))
            summed(chain, pick[:, :, :], lambda s: movestep[:, s, :])
            chain(v.tensor_tensor(place[:, :, :], pick[:, :, :], cellnum[:, :, :], ALU.add))
            chain(v.tensor_scalar(total[:, :], upto_b[:, :, NS - 1], float(-CAPC), 0.0, ALU.add, ALU.max))
            chain(v.tensor_scalar(ovc[:, :], total[:, :], 1.0 / CC, 0.5 - 0.5 / CC, ALU.mult, ALU.add))
            chain(v.tensor_scalar(ovc[:, :], ovc[:, :], MAGIC, MAGIC, ALU.add, ALU.subtract))
            chain(v.tensor_tensor_scan(ovend[:, :], ones[:, 0:NB], ovc[:, :], 0.0, ALU.mult, ALU.add))
            v.tensor_copy(nov[:, :], ovend[:, NB - 1:NB]).then_inc(s_nov, 1)
            dve.wait_ge(s_nov, 1)
            with dve.If(dve.value_load(nov[0:1, 0:1], min_val=0, max_val=OV) > 0):
                n = [0]

                def fix(ins):
                    n[0] += 1
                    ins.then_inc(s_fix, 1)
                    dve.wait_ge(s_fix, n[0])
                fix(v.tensor_tensor(delta[:, 0, :], ovend[:, :], ovc[:, :], ALU.subtract))
                fix(v.tensor_scalar(delta[:, 0, :], delta[:, 0, :], float(CC), float(OV0 - CAPC), ALU.mult, ALU.add))
                fix(v.scalar_tensor_tensor(delta[:, 0, :], iota_row[:, 0:NB], float(-CAPC), delta[:, 0, :], ALU.mult, ALU.add))
                v.tensor_copy(deltastep[:, 0:1], delta[:, 0, 0:1])
                v.tensor_scalar(deltastep[:, NB:NB + 1], delta[:, 0, NB - 1:NB], -1.0, None, ALU.mult)
                fix(v.tensor_tensor(deltastep[:, 1:NB], delta[:, 0, 1:NB], delta[:, 0, 0:NB - 1], ALU.subtract))
                fix(v.tensor_reduce(pick[:, :, :], at_least, AX.X, ALU.add))
                fix(v.scalar_tensor_tensor(pick[:, :, :], pick[:, :, :], float(-CAPC), place[:, :, :], ALU.mult, ALU.add))
                summed(fix, behind[:, :, :], lambda s: deltastep[:, :])
                fix(v.scalar_tensor_tensor(pick[:, :, :], pick[:, :, :], 0.0, behind[:, :, :], ALU.is_ge, ALU.mult))
                fix(v.tensor_tensor(place[:, :, :], place[:, :, :], pick[:, :, :], ALU.add))
                fix(v.memset(ovblk[:, :], 0.0))
                for b in range(NB - 1):
                    fix(v.scalar_tensor_tensor(ovblk[:, :], ovnum[:, :], ovend[0:1, b:b + 1], ovblk[:, :], ALU.is_ge, ALU.add))
                fix(v.tensor_copy(ovblk_i[:, :], ovblk[:, :]))
            v.memset(tmp1[:, 1, :], 0.0).then_inc(s_slots, 1)
            dve.wait_ge(s_amaxb, 1)
            chain(v.tensor_scalar(pw[:, :], ptr[:, 0:3], 1e-30, None, ALU.max))
            chain(v.tensor_single_scalar(pw[:, :].bitcast(i32), pw[:, :].bitcast(i32), 0x7F800000, ALU.bitwise_and))
            chain(v.tensor_scalar(ipw[:, :].bitcast(i32), pw[:, :].bitcast(i32), -1.0, float(0x7F000000), ALU.mult, ALU.add))
            v.tensor_scalar(fac[:, 0:1], ipw[:, 0:1], 2.0 ** 6, None, ALU.mult)
            v.tensor_scalar(fac[:, 1:2], ipw[:, 1:2], 2.0 ** 10, None, ALU.mult)
            v.tensor_scalar(fac[:, 2:3], ipw[:, 2:3], 2.0 ** 10, None, ALU.mult)
            v.tensor_scalar(fac[:, 3:4], pw[:, 1:2], 2.0 ** -20, None, ALU.mult)
            chain(v.tensor_scalar(fac[:, 4:5], pw[:, 0:1], pw[:, 2:3], 2.0 ** -16, ALU.mult, ALU.mult))
            v.memset(tmp1[:, 0, :], 0.0).then_inc(s_fac, 1)
            def low_rows(b, q):
                dve.wait_ge(s_hc, b + 1)
                v.scalar_tensor_tensor(hs[:, q, 1, :], py[q][:, 0:D], fac[:, 0:1], hs[:, q, 0, :], ALU.mult, ALU.subtract)\
                 .then_inc(s_hlo, 1)

            def batches(s, q):
                for i in range(BT):
                    n = s * BT + i
                    wait(dve, s_packed, n - 1)
                    v.tensor_tensor(hioh[:, i % 2, :, :], iota_row[:, None, 0:HI].to_broadcast([P, BW, HI]),
                                    hif[:, bass.ds(n * BW, BW)][:, :, None].to_broadcast([P, BW, HI]), ALU.is_equal).then_inc(s_hieq, 1)
                    wait(dve, s_sorted, n - 1)
                    v.tensor_tensor(laneoh[:, i % 2, :, :], iota_row[:, None, :].to_broadcast([P, BW, P]),
                                    lanef[:, bass.ds(n * BW, BW)][:, :, None].to_broadcast([P, BW, P]), ALU.is_equal)
                    dve.wait_ge(s_hieq, n + 1)
                    v.tensor_tensor(moving[:, i % 2, :, 1, :], hioh[:, i % 2, :, :],
                                    ew[:, bass.ds(n * BW, BW)][:, :, None].to_broadcast([P, BW, HI]), ALU.mult).then_inc(s_weighed, 1)
                    if i % 2 and i // 2 in beside(s):
                        h = s * HS + i // 2
                        if not isinstance(h, int) or h > 0:
                            low_rows(h - 1, 1 - i // 2 % 2)
            pairs(dve, batches, last=NS)

            low_rows(LB - 1, (LB - 1) % 2)
            dve.wait_ge(s_xpbready, 1)
            with dve.If(dve.value_load(nov[0:1, 0:1], min_val=0, max_val=OV) > 0):
                with dve.Fori(0, OV) as j:
                    dve.wait_ge(s_ovrec, j * 16 + 16)
                    v.tensor_copy(packi[:, 0, 0:1], recov[:, 0:1])
                    v.tensor_scalar(wh[:, 0, 0:1], recov[:, 1:2], fac[:, 2:3], None, ALU.mult).then_inc(s_ovw, 1)
                    dve.wait_ge(s_ovw, j * 3 + 1)
                    v.tensor_single_scalar(gidx[:, 0, 0:1], packi[:, 0, 0:1], 7, ALU.arith_shift_right).then_inc(s_ovidx, 1)
                    v.tensor_copy(wsc[:, 0, 0, 0:1], wh[:, 0, 0:1])
                    v.scalar_tensor_tensor(wsc[:, 0, 1, 0:1], recov[:, 1:2], fac[:, 2:3], wh[:, 0, 0:1], ALU.mult, ALU.subtract)
                    v.tensor_single_scalar(rowi[:, 0, 0:1], packi[:, 0, 0:1], P - 1, ALU.bitwise_and).then_inc(s_ovw, 1)
                    dve.wait_ge(s_ovw, j * 3 + 2)
                    v.tensor_copy(rowf[:, 0, 0:1], rowi[:, 0, 0:1]).then_inc(s_ovw, 1)
                    dve.wait_ge(s_ovw, j * 3 + 3)
                    for s in range(2):
                        v.tensor_scalar(S[:, 0, 0, s, :], iota_h[:, :], rowf[:, 0, 0:1], wsc[:, 0, s, 0:1], ALU.is_equal,
                                        ALU.mult).then_inc(s_ovS, 1)
                    dve.wait_ge(s_ovmm, j + 1)
                    ob = dve.value_load(ovblk_i[0:1, bass.ds(j, 1)], min_val=0, max_val=NB - 1)
                    v.scalar_tensor_tensor(xpb[:, bass.ds(ob, 1), :].rearrange("p a d -> p (a d)"), pmisc[:, 0:D], fac[:, 4:5],
                                           xpb[:, bass.ds(ob, 1), :].rearrange("p a d -> p (a d)"), ALU.mult, ALU.add)\
                     .then_inc(s_ovadd, 1)
                    dve.wait_ge(s_ovadd, j + 1)
                dve.wait_ge(s_ovadd, OV)
            PRE, ROUT = 2 + RS, 8
            sel, prep, rout = Chain(dve, s_sel), Chain(dve, s_prep), Chain(dve, s_rout)

            def take_apart(b, q):
                dve.wait_ge(s_rec[q], (b - q) * 8 + 16)
                sel.base, sel.n = SEL * b, 0
                weight = recb[:, q, :, 1]
                v.tensor_copy(packi[:, q, :], recb[:, q, :, 0])
                sel(v.tensor_scalar(wh[:, q, :], weight, fac[:, 2:3], None, ALU.mult))
                v.tensor_single_scalar(gidx[:, q, :], packi[:, q, :], 7, ALU.arith_shift_right).then_inc(s_gidx, 1)
                sel(v.tensor_single_scalar(rowi[:, q, :], packi[:, q, :], P - 1, ALU.bitwise_and))
                sel(v.tensor_copy(rowf[:, q, :], rowi[:, q, :]))
                v.tensor_copy(wsc[:, q, 0, :], wh[:, q, :])
                sel(v.scalar_tensor_tensor(wsc[:, q, 1, :], weight, fac[:, 2:3], wh[:, q, :], ALU.mult, ALU.subtract))
                assert sel.n == SEL
                wait(dve, s_mm, CH * (b - 1))

            def select(b, q, parts):
                for i in parts:
                    c, s = i // 2, i % 2
                    v.tensor_scalar(S[:, q, c, s, :], iota_h[:, :], rowf[:, q, c:c + 1],
                                    wsc[:, q, s, c:c + 1], ALU.is_equal, ALU.mult).then_inc(s_S, 1)

            def take_sum(b, q):
                dve.wait_ge(s_mm, CH * (b + 1))
                v.scalar_tensor_tensor(x1[:, q, :], pagg[q][:, 0:D], fac[:, 4:5], xpb[:, b, :], ALU.mult, ALU.add)\
                 .then_inc(s_x1, 1)

            def statistics(b, q):
                prep.base, prep.n = PRE * b, 0
                dve.wait_ge(s_x1, b + 1)
                prep(v.bn_stats(st[:, q, :], x1[:, q, :]))
                apart(dve)
                prep(v.bn_aggr(mv[:, q, :], st[:, q, :]))
                rsqrt_guess(prep, rstd[:, q, :], mv[:, q, 1:2], tmp1[:, q, :])

            def newton(b, q, n):
                newton_steps(prep, rstd[:, q, :], mv[:, q, 1:2], tmp1[:, q, :], n)

            def apply_norm(b, q):
                v.tensor_scalar(x2[:, q, :], x1[:, q, :], mv[:, q, 0:1], rstd[:, q, :], ALU.subtract, ALU.mult)\
                 .then_inc(s_x2, 1)
                assert prep.n == PRE

            def residual(b, q):
                rout.base, rout.n = ROUT * b, 0
                dve.wait_ge(s_x2, b + 1)
                wait(dve, s_out[q], (b - q) * 8)
                rout(v.tensor_tensor(acc[:, q, :], x1[:, q, :], x2[:, q, :], ALU.add))

            def probabilities(b, q):
                t = sm[:, q, :]
                dve.wait_ge(s_ex, b + 1)
                rout(v.reciprocal(t[:, 1:2], t[:, 2:3]))
                rout(v.tensor_scalar(t[:, 8:16], t[:, 16:24], t[:, 1:2], None, ALU.mult))
                apart(dve)
                rout(v.max(t[:, 24:32], t[:, 8:16]))
                apart(dve)
                v.max_index(idx8[:, q, :], t[:, 24:32], t[:, 8:16])
                rout(v.tensor_scalar(t[:, 3:4], t[:, 24:25], t[:, 25:26], 1e-12, ALU.add, ALU.max))
                v.tensor_copy(t[:, 4:6], idx8[:, q, 0:2])

            def combine(b, q):
                t = sm[:, q, :]
                rout(v.reciprocal(t[:, 6:7], t[:, 3:4]))
                rout(v.tensor_scalar(t[:, 32:34], t[:, 24:26], t[:, 6:7], None, ALU.mult))
                v.tensor_scalar(t[:, 40:48], iota_row[:, 0:NE], t[:, 4:5], t[:, 32:33], ALU.is_equal, ALU.mult)
                rout(v.tensor_scalar(t[:, 48:56], iota_row[:, 0:NE], t[:, 5:6], t[:, 33:34], ALU.is_equal, ALU.mult))
                v.tensor_tensor(t[:, 56:64], t[:, 40:48], t[:, 48:56], ALU.add).then_inc(s_comb, 1)
                assert rout.n == ROUT, rout.n

            def top_logit(b, q):
                dve.wait_ge(s_lgc, b + 1)
                v.reduce_max(sm[:, q, 0:1], lg[:, q, :], AX.X, negate=True).then_inc(s_mx, 1)

            def low_tokens(b, q):
                dve.wait_ge(s_x2Tc, 2 * (b + 1))
                v.scalar_tensor_tensor(x2p[:, q, 1, :, :].rearrange("p c n -> p (c n)"), x2T[:, q, :, :].rearrange("p c n -> p (c n)"),
                                       1024.0, x2p[:, q, 0, :, :].rearrange("p c n -> p (c n)"), ALU.mult, ALU.subtract)\
                 .then_inc(s_x2lo, 1)

            def add_bias(b, q):
                dve.wait_ge(s_yb, b + 1)
                dve.wait_ge(s_yacc, (NE + 1) * b + 3)
                v.tensor_tensor(acc[:, q, :], acc[:, q, :], pmisc[:, 256:512], ALU.add).then_inc(s_yacc, 1)

            def add_expert(b, q, e):
                if e == 0:
                    dve.wait_ge(s_comb, b + 1)
                dve.wait_ge(s_y, NE * b + e + 1)
                wait(dve, s_yacc, (NE + 1) * b + added(e))
                v.scalar_tensor_tensor(acc[:, q, :], py[e % 2][:, 0:D], sm[:, q, 56 + e:57 + e], acc[:, q, :],
                                       ALU.mult, ALU.add).then_inc(s_yacc, 1)

            take_apart(0, 0)
            select(0, 0, range(2 * CH))

            def turn(b, q, agg, mid, exp):
                ahead = agg and not (isinstance(b, int) and b + 1 == NB)
                todo = iter(range(2 * CH)) if ahead else iter(())

                def select_next(n=1):
                    select(b + 1, 1 - q, [i for _, i in zip(range(n), todo)])
                prep.between = lambda: select_next(prep.n % 2)
                rout.between = select_next
                for e in range(NE):
                    if mid and e == 3:
                        residual(b - 1, 1 - q)
                    if mid and e == 5:
                        low_tokens(b - 1, 1 - q)
                        top_logit(b - 1, 1 - q)
                    if mid and e == 2:
                        newton(b - 1, 1 - q, 2)
                        apply_norm(b - 1, 1 - q)
                    if exp:
                        add_expert(b - 2, q, e)
                    if exp and e == 2:
                        add_bias(b - 2, q)
                    if mid and e == 0:
                        take_sum(b - 1, 1 - q)
                    if ahead and e == 0:
                        take_apart(b + 1, 1 - q)
                    if mid and e == 0:
                        statistics(b - 1, 1 - q)
                    if mid and e == 1:
                        newton(b - 1, 1 - q, 1)
                    if mid and e == 6:
                        probabilities(b - 1, 1 - q)
                        combine(b - 1, 1 - q)
                    select_next(3)
                select_next(2 * CH)
            turn(0, 0, True, False, False)
            turn(1, 1, True, True, False)
            pairs(dve, lambda b, q: turn(b, q, True, True, True), first=2, last=NB - 1, steady=4)
            turn(NB - 1, (NB - 1) % 2, True, True, True)
            turn(NB, NB % 2, False, True, True)
            turn(NB + 1, (NB + 1) % 2, False, False, True)

        @block.scalar
        def _(act):
            a = nc.scalar
            act.wait_ge(s_x, 32)
            for b in range(LB):
                wait(act, s_sumx, b - 1)
                a.activation(xh[:, b % 2, :], xt[:, b, :], ACT.Copy, accum_out=sumx[:, b:b + 1]).then_inc(s_sumx, 1)
            act.wait_ge(s_sumx, LB)
            a.mul(minus_mean[:, :], sumx[:, :], -1.0 / D).then_inc(s_sumx, 1)
            act.wait_ge(s_sumx, LB + 1)
            for b in range(LB):
                wait(act, s_varx, b - 1)
                a.activation(xh[:, b % 2, :], xt[:, b, :], ACT.Square, bias=minus_mean[:, b:b + 1], scale=1.0,
                                   accum_out=varx[:, b:b + 1]).then_inc(s_varx, 1)
            act.wait_ge(s_varx, LB)
            act.wait_ge(s_setT, 1)
            a.copy(gb[:, :], ptr[:, 256:512]).then_inc(s_setC, 1)
            a.copy(rwT[:, :, :].rearrange("k c e -> k (c e)"), ptr[:, 64:64 + KC * NE]).then_inc(s_setC, 1)
            a.copy(b1T[:, :], ptr[:, 96:96 + NE * KC]).then_inc(s_setC, 1)

            def cells_out(s, q):
                act.wait_ge(s_sorted, BT * (s + 1))
                wait(act, s_scat[q], (s - q) * 8 * GR)
                a.copy(cellrow[:, q, :, :, :].rearrange("p g j w -> p w (g j)"),
                       pagg[q][:, 0:2 * HI].rearrange("p (w n) -> p w n", w=2)).then_inc(s_cells, 1)
                a.copy(placeof[:, q, :], place[:, bass.ds(s, 1), :].rearrange("p a g -> p (a g)")).then_inc(s_cells, 1)
            def norm(h, q):
                wait(act, s_xhT, h - 1)
                a.activation(xh[:, q, :], xt[:, bass.ds(h, 1), :].rearrange("p a d -> p (a d)"), ACT.Identity,
                             bias=shiftx[:, bass.ds(h, 1)], scale=rsx[:, bass.ds(h, 1)]).then_inc(s_xh, 1)

            def copy_rows(h, q):
                act.wait_ge(s_xhT, h + 1)
                wait(act, s_hp, h - 1)
                a.copy(xhT[:, q, :, :].rearrange("k c n -> k (c n)"), ph[q][:, 0:KC * P]).then_inc(s_xhTc, 1)

            def round_rows(h, q):
                act.wait_ge(s_hp, h + 1)
                wait(act, s_hst[q], (h - q) * 8)
                a.mul(hs[:, q, 0, :], py[q][:, 0:D], fac[:, 0:1]).then_inc(s_hc, 1)

            def span(s, q):
                for k in beside(s):
                    h = s * HS + k
                    copy_rows(h, k % 2)
                    if not isinstance(h, int) or h + 1 < LB:
                        norm(h + 1, 1 - k % 2)
                    if k == 0 and not (isinstance(s, int) and s == 0):
                        cells_out(s - 1, 1 - q)
                    round_rows(h, k % 2)
                    if isinstance(s, int) and s == 0 and k == 1:
                        a.mul(w1s, w1s, fac[:, 1:2]).then_inc(s_scaled, 1)
                    if isinstance(s, int) and s == 1 and k == 1:
                        act.wait_ge(s_scaled, 1)
                        act.wait_ge(s_zero, 16)
                        a.copy(w1p[:, 0, :, :, :].rearrange("p e c n -> p (e c) n"), w1s).then_inc(s_hi, 1)
            act.wait_ge(s_slots, 1)
            act.wait_ge(s_fac, 1)
            act.wait_ge(s_xnorm, 1)
            norm(0, 0)
            pairs(act, span, last=NS)
            cells_out(NS - 1, (NS - 1) % 2)

            def copy_tokens(b, q):
                act.wait_ge(s_x2T, b + 1)
                a.copy(x2T[:, q, :, :].rearrange("k c n -> k (c n)"), ptr[:, 0:KC * P]).then_inc(s_x2Tc, 1)
                a.mul(x2p[:, q, 0, :, :].rearrange("k c n -> k (c n)"), ptr[:, 0:KC * P], 1024.0).then_inc(s_x2Tc, 1)

            def copy_logits(b, q):
                act.wait_ge(s_lg, b + 1)
                a.copy(lg[:, q, :], pmisc[:, 0:NE]).then_inc(s_lgc, 1)

            def exponentials(b, q):
                act.wait_ge(s_mx, b + 1)
                a.activation(sm[:, q, 16:24], lg[:, q, :], ACT.Exp, bias=sm[:, q, 0:1], scale=1.0,
                             accum_out=sm[:, q, 2:3]).then_inc(s_ex, 1)

            def copy_weights(b, q):
                act.wait_ge(s_cT, b + 1)
                a.copy(combT[:, q, :], ptr[0:NE, 256:256 + P]).then_inc(s_cTc, 1)

            def hidden(b, e):
                act.wait_ge(s_h1, NE * b + e + 1)
                wait(act, s_y, NE * b + e - 1)
                for m in range(KC):
                    ins = a.activation(hT[:, e % 2, m, :], ph[e % 2][:, m * P:(m + 1) * P], ACT.Gelu,
                                       bias=b1T[:, e * KC + m:e * KC + m + 1], scale=fac[:, 3:4])
                ins.then_inc(s_gelu, 1)

            def turn(b, q, agg, mid, exp):
                for e in range(NE):
                    if mid and e == 4:
                        copy_tokens(b - 1, 1 - q)
                    if mid and e == 5:
                        copy_logits(b - 1, 1 - q)
                    if exp and e + 2 < NE:
                        hidden(b - 2, e + 2)
                    if exp and e == 1:
                        copy_weights(b - 2, q)
                    if mid and e + 2 >= NE:
                        hidden(b - 1, e + 2 - NE)
                    if mid and e == 5:
                        exponentials(b - 1, 1 - q)
            turns(act, turn)

        @block.tensor
        def _(pe):
            t = nc.tensor
            pe.wait_ge(s_const, 2)
            pe.wait_ge(s_w, 112)
            t.matmul(ptr[:, 256:512], lhsT=ones[0:1, :], rhs=gb_row[:, :], start=True, stop=True)
            for c in range(KC):
                t.transpose(ptr[:, 64 + c * NE:64 + (c + 1) * NE], rw_n[:, c * P:(c + 1) * P], ident[0:NE, 0:NE])
            t.transpose(ptr[:, 96:96 + NE * KC], b1n[:, :], ident[0:NE * KC, 0:NE * KC]).then_inc(s_setT, 1)

            pe.wait_ge(s_taken, NB)
            counts = cnt[:, :, :].rearrange("p b s -> p (b s)")
            t.matmul(pmisc[:, 0:NB * NS], lhsT=lower[:, :], rhs=counts, start=True, stop=True)
            t.matmul(pmisc[:, 256:256 + NB * NS], lhsT=ones[:, :], rhs=counts, start=True, stop=True).then_inc(s_base, 1)
            pe.wait_ge(s_setC, 3)
            pe.wait_ge(s_amax, 1)
            t.transpose(ptr[0:3, 0:P], amax[:, :], ident[:, :]).then_inc(s_amaxT, 1)
            pe.wait_ge(s_amaxd, 1)
            t.matmul(ptr[:, 0:3], lhsT=ones[0:3, :], rhs=amaxd[:, :], start=True, stop=True).then_inc(s_amaxb, 1)

            def transpose_rows(h, q):
                pe.wait_ge(s_xh, h + 1)
                wait(pe, s_xhTc, h - 1)
                for c in range(KC):
                    ins = t.transpose(ph[q][:, c * P:(c + 1) * P], xh[:, q, c * P:(c + 1) * P], ident[:, :])
                ins.then_inc(s_xhT, 1)

            def table_rows(h, q):
                pe.wait_ge(s_xhTc, h + 1)
                wait(pe, s_hlo, h - 1)
                for c in range(KC):
                    ins = t.matmul(py[q][:, 0:D], lhsT=xhT[:, q, c, :], rhs=gw[:, c, :], start=(c == 0), stop=(c == KC - 1))
                ins.then_inc(s_hp, 1)

            def sort(s, q):
                wait(pe, s_cells, 2 * (s - 1))
                for i in range(BT):
                    n = s * BT + i
                    pe.wait_ge(s_weighed, n + 1)
                    pe.wait_ge(s_packed, n + 1)
                    for c in range(BW):
                        ins = t.matmul(pagg[q][:, 0:2 * HI], lhsT=laneoh[:, i % 2, c, :],
                                       rhs=moving[:, i % 2, c, :, :].rearrange("p w n -> p (w n)"),
                                       start=(i == 0 and c == 0), stop=(i == BT - 1 and c == BW - 1))
                    ins.then_inc(s_sorted, 1)
                    if i // 2 in beside(s):
                        (table_rows if i % 2 else transpose_rows)(s * HS + i // 2, i // 2 % 2)
            pairs(pe, sort, last=NS)

            PARTS = ((0, 0), (0, 1), (1, 0))

            def sum_rows(psum, weights, rows, first, last):
                for n, (s, r) in enumerate(PARTS):
                    ins = t.matmul(psum, lhsT=weights[:, s, :], rhs=rows[:, r, :], start=(first and n == 0),
                                   stop=(last and n == len(PARTS) - 1))
                return ins

            def aggregate(b, q, chunks):
                for c in chunks:
                    if c == 0:
                        wait(pe, s_x1, b - 1)
                    pe.wait_ge(s_S, 2 * (CH * b + c + 1))
                    pe.wait_ge(s_G[c], (b + 1) * 16)
                    sum_rows(pagg[q][:, 0:D], S[:, q, c, :, :], G[:, c, :, :], c == 0, c == CH - 1).then_inc(s_mm, 1)

            def transpose_tokens(b, q):
                pe.wait_ge(s_x2, b + 1)
                wait(pe, s_cTc, b)
                for c in range(KC):
                    ins = t.transpose(ptr[:, c * P:(c + 1) * P], x2[:, q, c * P:(c + 1) * P], ident[:, :])
                ins.then_inc(s_x2T, 1)

            def logits(b, q):
                pe.wait_ge(s_x2Tc, b * 2 + 1)
                wait(pe, s_yacc, (NE + 1) * (b - 1) + 4)
                for c in range(KC):
                    ins = t.matmul(pmisc[:, 0:NE], lhsT=x2T[:, q, c, :], rhs=rwT[:, c, :], start=(c == 0), stop=(c == KC - 1))
                ins.then_inc(s_lg, 1)

            def transpose_weights(b, q):
                pe.wait_ge(s_comb, b + 1)
                t.transpose(ptr[0:NE, 256:256 + P], sm[:, q, 56:56 + NE], ident[:, :]).then_inc(s_cT, 1)

            def bias(b, q):
                pe.wait_ge(s_cTc, b + 1)
                t.matmul(pmisc[:, 256:512], lhsT=combT[:, q, :], rhs=b2s[:, :], start=True, stop=True).then_inc(s_yb, 1)

            def up(b, q, e):
                if e == 0:
                    pe.wait_ge(s_x2lo, b + 1)
                wait(pe, s_gelu, NE * b + e - 1)
                for m in range(KC):
                    n = 0
                    for c in range(KC):
                        for w, r in PARTS:
                            n += 1
                            ins = t.matmul(ph[e % 2][:, m * P:(m + 1) * P], lhsT=w1p[:, w, e, c, m * P:(m + 1) * P],
                                           rhs=x2p[:, q, r, c, :], start=(n == 1), stop=(n == KC * len(PARTS)))
                ins.then_inc(s_h1, 1)

            def down(b, q, e):
                pe.wait_ge(s_gelu, NE * b + e + 1)
                wait(pe, s_yacc, (NE + 1) * b + (added(e - 2) + 1 if e >= 2 else e - 1))
                for m in range(KC):
                    ins = t.matmul(py[e % 2][:, 0:D], lhsT=hT[:, e % 2, m, :], rhs=w2s[:, e * KC + m, :],
                                   start=(m == 0), stop=(m == KC - 1))
                ins.then_inc(s_y, 1)

            pe.wait_ge(s_xpbready, 1)
            pe.wait_ge(s_split, NE)
            pe.wait_ge(s_nov, 1)
            with pe.If(pe.value_load(nov[0:1, 0:1], min_val=0, max_val=OV) > 0):
                with pe.Fori(0, OV) as j:
                    pe.wait_ge(s_ovS, j * 2 + 2)
                    pe.wait_ge(s_ovG, j * 16 + 16)
                    sum_rows(pmisc[:, 0:D], S[:, 0, 0, :, :], G[:, 0, :, :], True, True).then_inc(s_ovmm, 1)
                    pe.wait_ge(s_ovadd, j + 1)
                pe.wait_ge(s_ovadd, OV)

            def turn(b, q, agg, mid, exp):
                for e in range(NE):
                    if agg:
                        aggregate(b, q, range(CH * e // NE, CH * (e + 1) // NE))
                    if mid and e == 4:
                        transpose_tokens(b - 1, 1 - q)
                    if mid and e == 5:
                        logits(b - 1, 1 - q)
                    if exp:
                        down(b - 2, q, e)
                    if exp and e + 2 < NE:
                        up(b - 2, q, e + 2)
                    if mid and e + 2 >= NE:
                        up(b - 1, 1 - q, e + 2 - NE)
                    if exp and e == 1:
                        transpose_weights(b - 2, q)
                    if exp and e == 2:
                        bias(b - 2, q)
            turns(pe, turn)


INPUTS = ["x", "src", "dst", "edge_weight", "L0_gnn_weight", "L0_gnn_b", "L0_ffn_router_w",
          "L0_ffn_w1", "L0_ffn_b1", "L0_ffn_w2", "L0_ffn_b2"]


def kernel(**inputs):
    import numpy as _np
    import concourse.bacc as _bacc
    from concourse import mybir as _mybir
    from concourse.bass_utils import run_bass_kernel_spmd as _run

    nc = _bacc.Bacc("TRN2", target_bir_lowering=False, num_devices=1)
    arrays, args = {}, []
    for name in INPUTS:
        a = _np.ascontiguousarray(inputs[name])
        arrays[f"in_{name}"] = a
        args.append(nc.dram_tensor(f"in_{name}", a.shape, _mybir.dt.from_np(a.dtype), kind="ExternalInput").ap())
    fp32 = _mybir.dt.float32
    out = nc.dram_tensor("out_0", (3125, 256), fp32, kind="ExternalOutput").ap()
    spans, cap, beyond, slots = room(arrays["in_src"].shape[0])
    cells = (BLOCKS * cap + beyond * 128) // CELL + spans * slots
    rec = nc.dram_tensor("rec_scratch", (cells, 2 * CELL), fp32, kind="Internal").ap()
    h = nc.dram_tensor("h_scratch", (3200, 512), _mybir.dt.float16, kind="Internal").ap()
    build_gnn_moe(nc, *args, out, rec, h)
    r = _run(nc, [arrays], core_ids=[0])
    return r.results[0]["out_0"]
```
